# Optimizing a Trainium2 kernel written in Bass

```python
import numpy as np
import jax
import jax.numpy as jnp

def _softmax(x, axis=-1):
    return jax.nn.softmax(x, axis=axis)

def _gelu(x):
    return jax.nn.gelu(x, approximate=True)

def _silu(x):
    return jax.nn.silu(x)

def _sigmoid(x):
    return jax.nn.sigmoid(x)

def _layernorm(x, axis=-1, eps=1e-05):
    m = jnp.mean(x, axis=axis, keepdims=True)
    v = jnp.var(x, axis=axis, keepdims=True)
    return (x - m) / jnp.sqrt(v + eps)

def _scatter_add(tgt, idx, src, axis=0):
    return tgt.at[idx].add(src)

def _segment_sum(src, seg, n):
    return jax.ops.segment_sum(src, seg, n)
kernel_name = 'mk_gnn_resnorm_d4_gnn_r16_afad52'

def setup_inputs(seed: int=0):
    np.random.seed(seed)
    _w = jnp.asarray

    def _rec_inputs():
        import jax
        import jax.numpy as jnp
        _gk = jax.random.key(seed)
        x = -0.0002928 + 1 * jax.random.normal(jax.random.fold_in(_gk, 1), (3125, 256), jnp.float32)
        _s = jax.random.randint(jax.random.fold_in(_gk, 2), (25000,), 0, 3125, jnp.int32)
        _d = jax.random.randint(jax.random.fold_in(_gk, 3), (25000,), 0, 3125, jnp.int32)
        _loop = jnp.arange(3125, dtype=jnp.int32)
        src = jnp.concatenate([_s, _d, _loop])
        dst = jnp.concatenate([_d, _s, _loop])
        _o = jnp.argsort(dst, stable=True)
        src = src[_o]
        dst = dst[_o]
        edge_attr_128 = -1.52775e-05 + 0.999936 * jax.random.normal(jax.random.fold_in(_gk, 12), (53125, 128), jnp.float32)
        return (x, src, dst, edge_attr_128)
    x, src, dst, edge_attr_128 = _rec_inputs()

    def _L0_gnn_setup():
        import jax, jax.numpy as jnp
        import numpy as np
        N_NODES = 1024
        N_EDGES = 16384
        D_NODE = 256
        D_EDGE = 128
        OUT_DIM = 256
        N_LAYERS = 3

        def _auto_mlp_dims(inp_dim, out_dim, n_layers):
            dims = np.logspace(np.log(inp_dim), np.log(out_dim), n_layers + 1, base=np.e)
            return [int(d) for d in np.round(dims)[1:]]

        def _segment_mean(data, seg, num_segments):
            s = jax.ops.segment_sum(data, seg, num_segments=num_segments, indices_are_sorted=True)
            c = jax.ops.segment_sum(jnp.ones((data.shape[0], 1), data.dtype), seg, num_segments=num_segments, indices_are_sorted=True)
            return s / jnp.maximum(c, 1.0)
        key = jax.random.key(seed)
        ks = jax.random.split(key, 12)
        n_embed = jax.random.normal(ks[0], (N_NODES, D_NODE), dtype=jnp.float32)
        e_embed = jax.random.normal(ks[1], (N_EDGES, D_EDGE), dtype=jnp.float32)
        senders = jnp.sort(jax.random.randint(ks[2], (N_EDGES,), 0, N_NODES))
        receivers = jax.random.randint(ks[3], (N_EDGES,), 0, N_NODES)
        dims = _auto_mlp_dims(2 * D_NODE, OUT_DIM, N_LAYERS)
        in_dims = [2 * D_NODE] + dims[:-1]
        params = {}
        for i, (di, do) in enumerate(zip(in_dims, dims)):
            params[f'W{i}'] = jax.random.normal(ks[4 + i], (di, do), dtype=jnp.float32) / np.sqrt(di)
            params[f'b{i}'] = jnp.zeros((do,), dtype=jnp.float32)
        params['Wg'] = jax.random.normal(ks[10], (D_EDGE, dims[-1]), dtype=jnp.float32) / np.sqrt(D_EDGE)
        return dict(n_embed=n_embed, e_embed=e_embed, senders=senders, receivers=receivers, **params)
    _L0_gnn_all = _L0_gnn_setup()
    _L0_gnn_in = {k: v for k, v in _L0_gnn_all.items() if k in ('W0', 'b0', 'W1', 'b1', 'W2', 'b2', 'Wg')}
    del _L0_gnn_all

    def _L1_gnn_setup():
        import jax, jax.numpy as jnp
        import numpy as np
        N_NODES = 3125
        N_EDGES = 50000
        D = 256

        def gcn_conv(x, edge_index, W, b, n_nodes):
            loops = jnp.arange(n_nodes, dtype=edge_index.dtype)
            src = jnp.concatenate([edge_index[0], loops])
            dst = jnp.concatenate([edge_index[1], loops])
            deg = jax.ops.segment_sum(jnp.ones_like(dst, dtype=x.dtype), dst, num_segments=n_nodes)
            dinv = jnp.where(deg > 0, jax.lax.rsqrt(deg), 0.0)
            norm = dinv[src] * dinv[dst]
            h = x @ W
            msg = h[src] * norm[:, None]
            out = jax.ops.segment_sum(msg, dst, num_segments=n_nodes)
            return out + b
        key = jax.random.key(seed)
        k1, k2, k3, k4 = jax.random.split(key, 4)
        x = jax.random.normal(k1, (N_NODES, D), dtype=jnp.float32)
        edge_index = jax.random.randint(k2, (2, N_EDGES), 0, N_NODES, dtype=jnp.int64)
        s = 1.0 / np.sqrt(D)
        W1 = jax.random.normal(k3, (D, D), dtype=jnp.float32) * s
        W2 = jax.random.normal(k4, (D, D), dtype=jnp.float32) * s
        b1 = jnp.zeros((D,), dtype=jnp.float32)
        b2 = jnp.zeros((D,), dtype=jnp.float32)
        return {'x': x, 'edge_index': edge_index, 'W1': W1, 'b1': b1, 'W2': W2, 'b2': b2}
    _L1_gnn_all = _L1_gnn_setup()
    _L1_gnn_in = {k: v for k, v in _L1_gnn_all.items() if k in ('W1', 'b1', 'W2', 'b2')}
    del _L1_gnn_all

    def _L2_gnn_setup():
        import jax, jax.numpy as jnp
        import numpy as np
        N_NODES = 3125
        N_EDGES = 50000
        D_IN = 256
        D_HID = 256
        D_OUT = 256

        def _sage_conv(x, src, dst, Wl, bl, Wr, num_nodes):
            msg = x[src]
            agg = jax.ops.segment_sum(msg, dst, num_segments=num_nodes)
            deg = jax.ops.segment_sum(jnp.ones((src.shape[0],), x.dtype), dst, num_segments=num_nodes)
            mean = agg / jnp.maximum(deg, 1.0)[:, None]
            return jnp.einsum('nd,od->no', mean, Wl) + bl + jnp.einsum('nd,od->no', x, Wr)
        key = jax.random.key(seed)
        ks = jax.random.split(key, 12)
        x = jax.random.normal(ks[0], (N_NODES, D_IN), dtype=jnp.float32)
        edge_index = jax.random.randint(ks[1], (2, N_EDGES), 0, N_NODES, dtype=jnp.int32)

        def lin(k, dout, din):
            return jax.random.normal(k, (dout, din), dtype=jnp.float32) * (1.0 / np.sqrt(din))
        return {'x': x, 'edge_index': edge_index, 'W1l': lin(ks[2], D_HID, D_IN), 'b1l': jnp.zeros((D_HID,), jnp.float32), 'W1r': lin(ks[3], D_HID, D_IN), 'W2l': lin(ks[4], D_HID, D_HID), 'b2l': jnp.zeros((D_HID,), jnp.float32), 'W2r': lin(ks[5], D_HID, D_HID), 'W3l': lin(ks[6], D_OUT, D_HID), 'b3l': jnp.zeros((D_OUT,), jnp.float32), 'W3r': lin(ks[7], D_OUT, D_HID)}
    _L2_gnn_all = _L2_gnn_setup()
    _L2_gnn_in = {k: v for k, v in _L2_gnn_all.items() if k in ('W1l', 'b1l', 'W1r', 'W2l', 'b2l', 'W2r', 'W3l', 'b3l', 'W3r')}
    del _L2_gnn_all

    def _L3_gnn_setup():
        import jax, jax.numpy as jnp
        import numpy as np
        N_NODES = 6250
        IN_FEATS = 256
        OUT_FEATS = 256
        N_EDGES = 200000
        key = jax.random.key(seed)
        k1, k2, k3, k4 = jax.random.split(key, 4)
        x = jax.random.normal(k1, (N_NODES, IN_FEATS), dtype=jnp.float32)
        edge_index = jax.random.randint(k2, (2, N_EDGES), 0, N_NODES, dtype=jnp.int64)
        scale = 1.0 / np.sqrt(IN_FEATS)
        W = jax.random.uniform(k3, (IN_FEATS, OUT_FEATS), dtype=jnp.float32, minval=-scale, maxval=scale)
        b = jax.random.uniform(k4, (OUT_FEATS,), dtype=jnp.float32, minval=-scale, maxval=scale)
        return {'x': x, 'edge_index': edge_index, 'W': W, 'b': b}
    _L3_gnn_all = _L3_gnn_setup()
    _L3_gnn_in = {k: v for k, v in _L3_gnn_all.items() if k in ('W', 'b')}
    del _L3_gnn_all
    return {'x': x, 'src': src, 'dst': dst, 'edge_attr_128': edge_attr_128, 'L0_gnn_W0': _L0_gnn_in['W0'], 'L0_gnn_b0': _L0_gnn_in['b0'], 'L0_gnn_W1': _L0_gnn_in['W1'], 'L0_gnn_b1': _L0_gnn_in['b1'], 'L0_gnn_W2': _L0_gnn_in['W2'], 'L0_gnn_b2': _L0_gnn_in['b2'], 'L0_gnn_Wg': _L0_gnn_in['Wg'], 'L1_gnn_W1': _L1_gnn_in['W1'], 'L1_gnn_b1': _L1_gnn_in['b1'], 'L1_gnn_W2': _L1_gnn_in['W2'], 'L1_gnn_b2': _L1_gnn_in['b2'], 'L2_gnn_W1l': _L2_gnn_in['W1l'], 'L2_gnn_b1l': _L2_gnn_in['b1l'], 'L2_gnn_W1r': _L2_gnn_in['W1r'], 'L2_gnn_W2l': _L2_gnn_in['W2l'], 'L2_gnn_b2l': _L2_gnn_in['b2l'], 'L2_gnn_W2r': _L2_gnn_in['W2r'], 'L2_gnn_W3l': _L2_gnn_in['W3l'], 'L2_gnn_b3l': _L2_gnn_in['b3l'], 'L2_gnn_W3r': _L2_gnn_in['W3r'], 'L3_gnn_W': _L3_gnn_in['W'], 'L3_gnn_b': _L3_gnn_in['b']}

def reference(x, src, dst, edge_attr_128, L0_gnn_W0, L0_gnn_b0, L0_gnn_W1, L0_gnn_b1, L0_gnn_W2, L0_gnn_b2, L0_gnn_Wg, L1_gnn_W1, L1_gnn_b1, L1_gnn_W2, L1_gnn_b2, L2_gnn_W1l, L2_gnn_b1l, L2_gnn_W1r, L2_gnn_W2l, L2_gnn_b2l, L2_gnn_W2r, L2_gnn_W3l, L2_gnn_b3l, L2_gnn_W3r, L3_gnn_W, L3_gnn_b):
    import jax
    import jax.numpy as jnp

    def _L0_gnn_ref(n_embed, e_embed, senders, receivers, W0, b0, W1, b1, W2, b2, Wg):
        import jax, jax.numpy as jnp
        import numpy as np
        N_NODES = 1024
        N_EDGES = 16384
        D_NODE = 256
        D_EDGE = 128
        OUT_DIM = 256
        N_LAYERS = 3

        def _auto_mlp_dims(inp_dim, out_dim, n_layers):
            dims = np.logspace(np.log(inp_dim), np.log(out_dim), n_layers + 1, base=np.e)
            return [int(d) for d in np.round(dims)[1:]]

        def _segment_mean(data, seg, num_segments):
            s = jax.ops.segment_sum(data, seg, num_segments=num_segments, indices_are_sorted=True)
            c = jax.ops.segment_sum(jnp.ones((data.shape[0], 1), data.dtype), seg, num_segments=num_segments, indices_are_sorted=True)
            return s / jnp.maximum(c, 1.0)
        h = jnp.concatenate([n_embed[senders], n_embed[receivers]], axis=-1)
        h = jnp.tanh(h @ W0 + b0)
        h = jnp.tanh(h @ W1 + b1)
        h = h @ W2 + b2
        h = h * (e_embed @ Wg)
        return _segment_mean(h, senders, n_embed.shape[0])

    def _L1_gnn_ref(x, edge_index, W1, b1, W2, b2):
        import jax, jax.numpy as jnp
        import numpy as np
        N_NODES = 3125
        N_EDGES = 50000
        D = 256

        def gcn_conv(x, edge_index, W, b, n_nodes):
            loops = jnp.arange(n_nodes, dtype=edge_index.dtype)
            src = jnp.concatenate([edge_index[0], loops])
            dst = jnp.concatenate([edge_index[1], loops])
            deg = jax.ops.segment_sum(jnp.ones_like(dst, dtype=x.dtype), dst, num_segments=n_nodes)
            dinv = jnp.where(deg > 0, jax.lax.rsqrt(deg), 0.0)
            norm = dinv[src] * dinv[dst]
            h = x @ W
            msg = h[src] * norm[:, None]
            out = jax.ops.segment_sum(msg, dst, num_segments=n_nodes)
            return out + b
        n = x.shape[0]
        out = gcn_conv(x, edge_index, W1, b1, n)
        out = jax.nn.relu(out)
        out = out + gcn_conv(x, edge_index, W2, b2, n)
        return out

    def _L2_gnn_ref(x, edge_index, W1l, b1l, W1r, W2l, b2l, W2r, W3l, b3l, W3r):
        import jax, jax.numpy as jnp
        import numpy as np
        N_NODES = 3125
        N_EDGES = 50000
        D_IN = 256
        D_HID = 256
        D_OUT = 256

        def _sage_conv(x, src, dst, Wl, bl, Wr, num_nodes):
            msg = x[src]
            agg = jax.ops.segment_sum(msg, dst, num_segments=num_nodes)
            deg = jax.ops.segment_sum(jnp.ones((src.shape[0],), x.dtype), dst, num_segments=num_nodes)
            mean = agg / jnp.maximum(deg, 1.0)[:, None]
            return jnp.einsum('nd,od->no', mean, Wl) + bl + jnp.einsum('nd,od->no', x, Wr)
        src, dst = (edge_index[0], edge_index[1])
        n = x.shape[0]
        h = _sage_conv(x, src, dst, W1l, b1l, W1r, n)
        h = jax.nn.relu(h)
        h = _sage_conv(h, src, dst, W2l, b2l, W2r, n)
        h = jax.nn.relu(h)
        h = _sage_conv(h, src, dst, W3l, b3l, W3r, n)
        return h

    def _L3_gnn_ref(x, edge_index, W, b):
        import jax, jax.numpy as jnp
        import numpy as np
        N_NODES = 6250
        IN_FEATS = 256
        OUT_FEATS = 256
        N_EDGES = 200000
        n = x.shape[0]
        row = edge_index[0]
        col = edge_index[1]
        h = x @ W + b
        agg = jax.ops.segment_sum(h[col], row, num_segments=n)
        deg = jax.ops.segment_sum(jnp.ones((edge_index.shape[1],), dtype=h.dtype), row, num_segments=n)
        inv_deg = jnp.where(deg > 0, 1.0 / jnp.where(deg > 0, deg, 1.0), 0.0)
        return agg * inv_deg[:, None]
    edge_index = jnp.stack([src, dst])
    x = _layernorm(x + _L0_gnn_ref(x, edge_attr_128, src, dst, L0_gnn_W0, L0_gnn_b0, L0_gnn_W1, L0_gnn_b1, L0_gnn_W2, L0_gnn_b2, L0_gnn_Wg), axis=-1)
    x = _layernorm(x + _L1_gnn_ref(x, edge_index, L1_gnn_W1, L1_gnn_b1, L1_gnn_W2, L1_gnn_b2), axis=-1)
    x = _layernorm(x + _L2_gnn_ref(x, edge_index, L2_gnn_W1l, L2_gnn_b1l, L2_gnn_W1r, L2_gnn_W2l, L2_gnn_b2l, L2_gnn_W2r, L2_gnn_W3l, L2_gnn_b3l, L2_gnn_W3r), axis=-1)
    x = _layernorm(x + _L3_gnn_ref(x, edge_index, L3_gnn_W, L3_gnn_b), axis=-1)
    return x

_drawn_inputs = setup_inputs


def setup_inputs(seed=0):
    import zlib

    import numpy as np

    out = dict(_drawn_inputs(seed))
    spreads = {'L0_gnn_b0': (0.0, 0.692),
     'L0_gnn_b1': (0.0, 0.443),
     'L0_gnn_b2': (0.0, 0.356),
     'L1_gnn_b1': (0.0, 0.1),
     'L1_gnn_b2': (0.0, 0.1),
     'L2_gnn_b1l': (0.0, 0.1),
     'L2_gnn_b2l': (0.0, 0.1),
     'L2_gnn_b3l': (0.0, 0.1)}
    factors = {}
    for name, (base, spread) in spreads.items():
        noise = np.random.default_rng([zlib.crc32(name.encode()), seed]).standard_normal(out[name].shape)
        drawn = base * np.exp(spread * noise) if base else spread * noise
        out[name] = jnp.asarray(drawn.astype(out[name].dtype))
    for name, factor in factors.items():
        out[name] = (out[name] * factor).astype(out[name].dtype)
    return out
```

```python
from contextlib import ExitStack

import concourse.bass as bass
from concourse import mybir

F32 = mybir.dt.float32
I32 = mybir.dt.int32
ALU = mybir.AluOpType
ACT = mybir.ActivationFunctionType

P = 128
NODES = 3125
T = 25
NP = P * T
D = 256
KD = D // P
C = 128
GC = 4
G = 104
EP = G * GC * C
H1, H1T, H1P = 408, 4, 102
H2, H2T, H2P = 324, 3, 108
SW = D + 1
B = 5
TB = T // B
BW = TB * P
NW = BW // 2
CELLS = NP * NP
EPS = 1e-5
ZW = 13 * SW


def wait(eng, sem, value):
    if not (isinstance(value, int) and value <= 0):
        eng.wait_ge(sem, value)


class Chain:

    def __init__(self, eng, sem):
        self.eng, self.sem, self.base, self.n = eng, sem, 0, 0

    def start(self, base):
        self.base, self.n = base, 0

    def link(self, ins):
        self.n += 1
        ins.then_inc(self.sem, 1)
        wait(self.eng, self.sem, self.base + self.n)


def stand_alone(eng, s_up):
    eng.sem_inc(s_up)


def looped(eng, n, body, head=1, tail=1):
    for i in range(head):
        body(i)
    with eng.Fori(head, n - tail) as i:
        body(i)
    for i in range(n - tail, n):
        body(i)


def layer_norm_stats(v, ch, src, stats, mv, std, eps_t):
    ch.link(v.bn_stats(stats, src))
    stand_alone(v, s_up)
    ch.link(v.bn_aggr(mv, stats))


def build(nc, xT, x, src_col, dst_col, edge_T, W0, b0, W1, b1, W2b, Wg, gW, gb1, gb2, Wl, bl, Wr, W3, b3, out):
    ctx = ExitStack()
    with ctx:
        def sb(name, shape, dt=F32, c=ctx):
            return c.enter_context(nc.sbuf_tensor(name, shape, dt))

        def sem(name, c=ctx):
            return c.enter_context(nc.semaphore(name))

        def dram(name, shape):
            return nc.dram_tensor(name, shape, F32)

        p_tab, q_tab = dram("p_tab", [NP, H1]), dram("q_tab", [NP, H1])
        sums = dram("sums", [NP + P, SW])
        counts = dram("counts", [CELLS + P, 1])
        sums_v = sums[0:NP, :].rearrange("(p a) w -> p a w", p=P)
        counts_v = counts[0:CELLS, :].rearrange("(b p a c) o -> b p a (c o)", b=B, p=P, a=T)
        x_v = x.rearrange("(p a) c -> p a c", p=P)
        out_v = out.rearrange("(p a) c -> p a c", a=T)

        psum = [ctx.enter_context(nc.psum_tensor(f"bank{i}", [P, 512], F32)) for i in range(8)]

        s_up = sem("s_up")
        ident = sb("ident", [P, P])
        lower = sb("lower", [P, P])
        degree = sb("degree", [P, T])
        ones_row = sb("ones_row", [P, T])
        cnt_src = sb("cnt_src", [P, T])
        inv_src = sb("inv_src", [P, T])
        inv_dst = sb("inv_dst", [P, T])
        dinv = sb("dinv", [P, T])

        with ExitStack() as ec:
            def esb(name, shape, dt=F32):
                return sb(name, shape, dt, ec)

            def esem(name):
                return sem(name, ec)

            src_i = esb("src_i", [P, G * GC], I32)
            dst_i = esb("dst_i", [P, G * GC], I32)
            cells = esb("cells", [P, G * GC, 2])
            digits = esb("digits", [P, G * GC, 2])
            iota_p = esb("iota_p", [P, P])
            trash = esb("trash", [P, 2])
            w1 = esb("w1", [H1P, H1T, H2])
            w2 = esb("w2", [H2P, H2T, D])
            wg = esb("wg", [P, D])
            b1c = esb("b1c", [H2P, H2T])
            hidden1 = esb("hidden1", [H1P, H1T, GC * C])
            hidden2 = esb("hidden2", [H2P, H2T, GC * C])

            with ExitStack() as sc:
                def ssb(name, shape, dt=F32):
                    return sb(name, shape, dt, sc)

                def ssem(name):
                    return sem(name, sc)

                zeros = ssb("zeros", [P, ZW])
                w0 = ssb("w0", [P, 2 * KD, H1])
                b0_b = ssb("b0_b", [P, H1])
                xt = ssb("xt", [P, TB, KD, P])
                p_out = ssb("p_out", [P, TB, H1])
                q_out = ssb("q_out", [P, TB, H1])
                sf = ssb("sf", [P, G * GC])
                df = ssb("df", [P, G * GC])
                qi = ssb("qi", [P, G * GC], I32)
                qf = ssb("qf", [P, G * GC])
                rf = ssb("rf", [P, G * GC])
                mf = ssb("mf", [P, G * GC])
                s_zero, s_zd, s_w, s_idx = ssem("s_zero"), ssem("s_zd"), ssem("s_w"), ssem("s_idx")
                s_c, s_cg, s_cd = ssem("s_c"), ssem("s_cg"), ssem("s_cd")
                s_pq, s_pe, s_qe = ssem("s_pq"), ssem("s_pe"), ssem("s_qe")
                s_xt = [ssem(f"s_xt{j}") for j in range(TB)]
                s_po = [ssem(f"s_po{j}") for j in range(TB)]
                s_qo = [ssem(f"s_qo{j}") for j in range(TB)]
                s_wl = ssem("s_wl")
                n_zero = CELLS // (P * 3200)
                xT_v = xT.rearrange("(k p) n -> p k n", p=P)
                block = sc.enter_context(nc.Block())

                @block.sync
                def _(sp):
                    sp.dma_start(src_i[:], src_col).then_inc(s_idx, 16)
                    sp.dma_start(dst_i[:], dst_col).then_inc(s_idx, 16)
                    sp.dma_start(w0[:], W0.rearrange("(k p) n -> p k n", p=P)).then_inc(s_w, 16)
                    sp.dma_start(b0_b[:], b0.broadcast_to([P, H1])).then_inc(s_w, 16)

                    def body(b):
                        for j in range(TB):
                            n = b * TB + j
                            wait(sp, s_pq, n - TB + 1)
                            sp.dma_start(xt[:, j], xT_v[:, :, bass.ds(n * P, P)]).then_inc(s_xt[j], 16)
                        for j in range(TB):
                            n = b * TB + j
                            sp.wait_ge(s_pe, n + 1)
                            sp.dma_start(p_tab[bass.ds(n * P, P), :], p_out[:, j]).then_inc(s_po[j], 16)
                            sp.wait_ge(s_qe, n + 1)
                            sp.dma_start(q_tab[bass.ds(n * P, P), :], q_out[:, j]).then_inc(s_qo[j], 16)
                    looped(sp, B, body)
                    for j in range(TB):
                        sp.wait_ge(s_po[j], 16 * B)
                        sp.wait_ge(s_qo[j], 16 * B)

                @block.tensor
                def _(pe):
                    pe.wait_ge(s_w, 32)

                    def body(b):
                        for j in range(TB):
                            n = b * TB + j
                            pe.wait_ge(s_xt[j], 16 * (b + 1))
                            last = n - 1 if j == 0 else n - 4
                            if j in (0, 4) or not isinstance(b, int) or b > 0:
                                before = {0: n - 1, 4: n - 4}.get(j, n - TB)
                                wait(pe, s_pe, before + 1)
                                wait(pe, s_qe, before + 1)
                            for half in range(2):
                                for k in range(KD):
                                    mm = pe.matmul(psum[2 * (j % 4) + half][:, 0:H1], xt[:, j, k], w0[:, 2 * half + k],
                                                   start=(k == 0), stop=(k == KD - 1))
                            mm.then_inc(s_pq, 1)
                    looped(pe, B, body)

                @block.scalar
                def _(act):
                    act.wait_ge(s_zero, 1)
                    flat = counts[0:CELLS, :].rearrange("(m p c) o -> m p (c o)", p=P, c=3200)
                    for m in range(n_zero):
                        act.dma_start(flat[m], zeros[:, 0:3200]).then_inc(s_zd, 16)
                    act.dma_start(counts[CELLS:CELLS + P, :], zeros[:, 0:1]).then_inc(s_zd, 16)
                    for m in range(2):
                        act.dma_start(sums[m * 1664:(m + 1) * 1664, :].rearrange("(p a) w -> p (a w)", p=P),
                                      zeros[:]).then_inc(s_zd, 16)
                    act.dma_start(w1[:], W1.rearrange("(k p) n -> p k n", p=H1P)).then_inc(s_wl, 16)
                    act.dma_start(w2[:], W2b.rearrange("(k p) n -> p k n", p=H2P)).then_inc(s_wl, 16)
                    act.dma_start(wg[:], Wg).then_inc(s_wl, 16)
                    act.dma_start(b1c[:], b1).then_inc(s_wl, 16)

                    def body(b):
                        for j in range(TB):
                            n = b * TB + j
                            act.wait_ge(s_pq, n + 1)
                            wait(act, s_po[j], 16 * b)
                            act.copy(p_out[:, j], psum[2 * (j % 4)][:, 0:H1]).then_inc(s_pe, 1)
                    looped(act, B, body)
                    act.wait_ge(s_zd, 16 * (n_zero + 3))
                    act.wait_ge(s_wl, 64)

                @block.gpsimd
                def _(pool):
                    pool.memset(ident[:], 0.0).then_inc(s_cg, 1)
                    pool.memset(lower[:], 1.0).then_inc(s_cg, 1)
                    pool.wait_ge(s_cg, 2)
                    pool.affine_select(out=ident[:], in_=ident[:], compare_op=ALU.not_equal, fill=1.0, base=0,
                                       pattern=[[-1, P]], channel_multiplier=1).then_inc(s_cg, 1)
                    pool.affine_select(out=lower[:], in_=lower[:], compare_op=ALU.is_gt, fill=0.0, base=0,
                                       pattern=[[-1, P]], channel_multiplier=1).then_inc(s_cg, 1)
                    pool.iota(iota_p[:], [[1, P]], base=0, channel_multiplier=0,
                              allow_small_or_imprecise_dtypes=True).then_inc(s_cg, 1)
                    pool.iota(trash[:, 0:1], [[0, 1]], base=NP, channel_multiplier=1,
                              allow_small_or_imprecise_dtypes=True).then_inc(s_cg, 1)
                    pool.iota(trash[:, 1:2], [[0, 1]], base=CELLS, channel_multiplier=1,
                              allow_small_or_imprecise_dtypes=True).then_inc(s_cg, 1)
                    pool.wait_ge(s_cg, 7)

                @block.vector
                def _(v):
                    v.memset(zeros[:], 0.0).then_inc(s_zero, 1)
                    v.memset(degree[:], 0.0).then_inc(s_c, 1)
                    v.memset(hidden2[:], 1.0).then_inc(s_c, 1)
                    ch = Chain(v, s_cd)
                    v.wait_ge(s_idx, 32)
                    ch.link(v.tensor_copy(df[:], dst_i[:]))
                    ch.link(v.tensor_copy(sf[:], src_i[:]))
                    ch.link(v.tensor_scalar(qi[:], df[:], 1.0 / T, -0.48, ALU.mult, ALU.add))
                    ch.link(v.tensor_copy(qf[:], qi[:]))
                    ch.link(v.scalar_tensor_tensor(rf[:], qf[:], -float(T), df[:], ALU.mult, ALU.add))
                    ch.link(v.tensor_scalar(mf[:], rf[:], float(T), None, ALU.is_ge))
                    ch.link(v.tensor_tensor(qf[:], qf[:], mf[:], ALU.add))
                    ch.link(v.scalar_tensor_tensor(rf[:], mf[:], -float(T), rf[:], ALU.mult, ALU.add))
                    ch.link(v.tensor_scalar(mf[:], rf[:], 0.0, None, ALU.is_lt))
                    ch.link(v.tensor_tensor(qf[:], qf[:], mf[:], ALU.subtract))
                    ch.link(v.scalar_tensor_tensor(rf[:], mf[:], float(T), rf[:], ALU.mult, ALU.add))
                    ch.link(v.tensor_copy(digits[:, :, 0], qf[:]))
                    ch.link(v.tensor_copy(digits[:, :, 1], rf[:]))
                    ch.link(v.scalar_tensor_tensor(qf[:], rf[:], float(P), qf[:], ALU.mult, ALU.add))
                    ch.link(v.scalar_tensor_tensor(qf[:], sf[:], float(BW), qf[:], ALU.mult, ALU.add))
                    for k in range(1, B):
                        ch.link(v.tensor_scalar(mf[:], rf[:], float(TB * k), float((NP - 1) * BW), ALU.is_ge, ALU.mult))
                        ch.link(v.tensor_tensor(qf[:], qf[:], mf[:], ALU.add))
                    ch.link(v.tensor_copy(cells[:, :, 0], sf[:]))
                    ch.link(v.tensor_copy(cells[:, :, 1], qf[:]))
                    v.wait_ge(s_w, 32)

                    def body(b):
                        for j in range(TB):
                            n = b * TB + j
                            v.wait_ge(s_pq, n + 1)
                            wait(v, s_qo[j], 16 * b)
                            v.tensor_tensor(q_out[:, j], psum[2 * (j % 4) + 1][:, 0:H1], b0_b[:],
                                            ALU.add).then_inc(s_qe, 1)
                    looped(v, B, body)

            p_in = esb("p_in", [P, GC, H1])
            q_in = esb("q_in", [P, GC, H1])
            pre1 = esb("pre1", [P, GC, H1])
            gidx = esb("gidx", [P, 2, GC], I32)
            keys = esb("keys", [P, GC, 2])
            eT = esb("eT", [P, GC * C])
            same = esb("same", [P, GC, C])
            junk = esb("junk", [P, GC, C])
            junk2 = esb("junk2", [P, GC, C])
            junk3 = esb("junk3", [P, GC, C])
            before = esb("before", [P, GC, 2])
            number = esb("number", [P, GC])
            later = esb("later", [P, GC, 2])
            away = esb("away", [P, GC, 2])
            oh_p = esb("oh_p", [P, GC, P])
            oh_t = esb("oh_t", [P, GC, T])
            gated = esb("gated", [P, GC, D])
            msg = esb("msg", [P, GC, SW])
            msum = esb("msum", [P, GC, SW])
            number_out = esb("number_out", [P, GC])
            sidx = esb("sidx", [P, GC, 2], I32)

            s_gp = [esem(f"s_gp{c}") for c in range(GC)]
            s_gq = [esem(f"s_gq{c}") for c in range(GC)]
            s_idx = esem("s_gidx")
            s_add = esem("s_add")
            s_T = esem("s_T")
            s_th1 = esem("s_th1")
            s_L1 = esem("s_L1")
            s_th2 = esem("s_th2")
            s_L2 = esem("s_L2")
            s_gt = esem("s_gt")
            s_msg = esem("s_msg")
            s_S = esem("s_S")
            s_sev = esem("s_sev")
            s_MR = esem("s_MR")
            s_M = esem("s_M")
            s_oh = esem("s_oh")
            s_dmm = esem("s_dmm")
            s_dg = esem("s_dg")
            s_ks = esem("s_ks")
            s_fin = esem("s_fin")
            s_sums = esem("s_sums")
            s_cnt = esem("s_cnt")
            s_eT = esem("s_eT")
            s_vc = esem("s_vc")
            s_one = esem("s_one")
            bT, bH, bO, bM = psum[0:2], psum[2:4], psum[4:6], psum[6:8]
            blk = ec.enter_context(nc.Block())

            def edge_loop(eng, body):
                body(0, True, False)
                body(1, True, True)
                with eng.Fori(2, G) as g:
                    body(g, True, True)
                body(G, False, True)

            @blk.sync
            def _(sp):
                def body(g, front, back):
                    if front:
                        wait(sp, s_L2, g * GC)
                        sp.dma_start(eT[:], edge_T[:, bass.ds(g * (GC * C), GC * C)]).then_inc(s_eT, 16)
                edge_loop(sp, body)

            @blk.gpsimd
            def _(pool):
                def gather(g):
                    pool.wait_ge(s_idx, g + 1)
                    stand_alone(pool, s_up)
                    for c in range(GC):
                        pool.indirect_dma_start(out=p_in[:, c], out_offset=None, in_=p_tab[:],
                                                in_offset=bass.IndirectOffsetOnAxis(ap=gidx[:, 0, c:c + 1], axis=0)
                                                ).then_inc(s_gp[c], 16)
                        pool.indirect_dma_start(out=q_in[:, c], out_offset=None, in_=q_tab[:],
                                                in_offset=bass.IndirectOffsetOnAxis(ap=gidx[:, 1, c:c + 1], axis=0)
                                                ).then_inc(s_gq[c], 16)

                def body(g, front, back):
                    if front and not (isinstance(g, int) and g == G - 1):
                        gather(g + 1)
                    if back:
                        for c in range(GC):
                            n = (g - 1) * GC + c
                            if c == 0:
                                pool.wait_ge(s_fin, g)
                            wait(pool, s_cnt, 16 * n)
                            stand_alone(pool, s_up)
                            pool.indirect_dma_start(out=counts[:], in_=number_out[:, c:c + 1], in_offset=None,
                                                    out_offset=bass.IndirectOffsetOnAxis(ap=sidx[:, c, 1:2], axis=0),
                                                    compute_op=ALU.add).then_inc(s_cnt, 16)
                            pool.wait_ge(s_sev, n + 1)
                            wait(pool, s_sums, 16 * n)
                            stand_alone(pool, s_up)
                            pool.indirect_dma_start(out=sums[:], in_=msum[:, c], in_offset=None,
                                                    out_offset=bass.IndirectOffsetOnAxis(ap=sidx[:, c, 0:1], axis=0),
                                                    compute_op=ALU.add).then_inc(s_sums, 16)
                gather(0)
                body(0, True, False)
                body(1, True, True)
                with pool.Fori(2, G - 1) as g:
                    body(g, True, True)
                body(G - 1, True, True)
                body(G, False, True)
                pool.wait_ge(s_sums, 16 * G * GC)
                pool.wait_ge(s_cnt, 16 * G * GC)

            @blk.tensor
            def _(pe):
                def body(g, front, back):
                    if front:
                        for c in range(GC):
                            n = g * GC + c
                            pe.wait_ge(s_add, n + 1)
                            wait(pe, s_th1, n - 1)
                            for k in range(H1T):
                                mm = pe.transpose(bT[c % 2][0:H1P, k * C:(k + 1) * C],
                                                  pre1[:, c, k * H1P:(k + 1) * H1P], ident[:])
                            mm.then_inc(s_T, 1)
                    if back:
                        pe.wait_ge(s_ks, g)
                        for c in range(GC):
                            n = (g - 1) * GC + c
                            wait(pe, s_M, n - 1)
                            if c == 1:
                                wait(pe, s_dg, g - 1)
                            for s in range(2):
                                mm = pe.transpose(bM[c % 2][:, s * C:(s + 1) * C],
                                                  keys[:, c, s:s + 1].broadcast_to([P, P]), ident[:])
                            mm.then_inc(s_MR, 1)
                        pe.wait_ge(s_th2, H2T * g)
                        pe.wait_ge(s_eT, 16 * g)
                        for c in range(GC):
                            n = (g - 1) * GC + c
                            if c < 2:
                                wait(pe, s_sev, n - 1)
                            else:
                                pe.wait_ge(s_msg, n - 1)
                            e = slice(c * C, (c + 1) * C)
                            for k in range(H2T):
                                pe.matmul(bO[c % 2][:, 0:D], hidden2[:, k, e], w2[:, k],
                                          start=(k == 0), stop=(k == H2T - 1))
                            pe.matmul(bO[c % 2][:, D:2 * D], eT[:, e], wg[:], start=True, stop=True).then_inc(s_L2, 1)
                    if front:
                        pe.wait_ge(s_th1, (g + 1) * GC)
                        for m in range(H2T):
                            wait(pe, s_th2, H2T * g + m - 1 if m == 2 else H2T * g)
                            for k in range(H1T):
                                mm = pe.matmul(bH[m % 2][0:H2P, :], w1[:, k, m * H2P:(m + 1) * H2P], hidden1[:, k],
                                               start=(k == 0), stop=(k == H1T - 1))
                            mm.then_inc(s_L1, 1)
                    if back:
                        pe.wait_ge(s_oh, g)
                        pe.wait_ge(s_M, g * GC)
                        for c in range(GC):
                            mm = pe.matmul(bM[1][:, D:D + T], oh_p[:, c], oh_t[:, c], start=(c == 0), stop=(c == GC - 1))
                        mm.then_inc(s_dmm, 1)
                        pe.wait_ge(s_msg, g * GC)
                        for c in range(GC):
                            n = (g - 1) * GC + c
                            if c >= 2:
                                pe.wait_ge(s_sev, n - 1)
                            pe.matmul(bO[c % 2][:, 0:SW], same[:, c], msg[:, c], start=True, stop=True).then_inc(s_S, 1)
                edge_loop(pe, body)

            @blk.scalar
            def _(act):
                def body(g, front, back):
                    if front:
                        wait(act, s_L1, H2T * g)
                        for c in range(GC):
                            n = g * GC + c
                            act.wait_ge(s_T, n + 1)
                            act.activation(hidden1[:, :, c * C:(c + 1) * C],
                                           bT[c % 2][0:H1P, :].rearrange("p (k e) -> p k e", k=H1T),
                                           ACT.Tanh).then_inc(s_th1, 1)
                    if back:
                        for c in range(GC):
                            n = (g - 1) * GC + c
                            act.wait_ge(s_L2, n + 1)
                            wait(act, s_msg, n - GC + 1)
                            act.copy(gated[:, c], bO[c % 2][:, 0:D]).then_inc(s_gt, 1)
                    if front:
                        wait(act, s_L2, GC * g)
                        for m in range(H2T):
                            rows = H2P - 1 if m == H2T - 1 else H2P
                            act.wait_ge(s_L1, H2T * g + m + 1)
                            act.activation(hidden2[0:rows, m], bH[m % 2][0:rows, :], ACT.Tanh,
                                           bias=b1c[0:rows, m:m + 1]).then_inc(s_th2, 1)
                    if back:
                        for c in range(GC):
                            n = (g - 1) * GC + c
                            act.wait_ge(s_S, n + 1)
                            wait(act, s_sums, 16 * (n - GC + 1))
                            act.copy(msum[:, c], bO[c % 2][:, 0:SW]).then_inc(s_sev, 1)
                edge_loop(act, body)

            @blk.vector
            def _(v):
                ch = Chain(v, s_vc)
                per_group = 4

                def rows(g):
                    v.tensor_copy(gidx[:, 0], src_i[:, bass.ds(g * GC, GC)])
                    v.tensor_copy(gidx[:, 1], dst_i[:, bass.ds(g * GC, GC)]).then_inc(s_idx, 1)

                def body(g, front, back):
                    if front:
                        for c in range(GC):
                            n = g * GC + c
                            v.wait_ge(s_gp[c], 16 * (g + 1))
                            v.wait_ge(s_gq[c], 16 * (g + 1))
                            wait(v, s_T, n - GC + 1)
                            v.tensor_tensor(pre1[:, c], p_in[:, c], q_in[:, c], ALU.add).then_inc(s_add, 1)
                        if not (isinstance(g, int) and g == G - 1):
                            v.wait_ge(s_add, (g + 1) * GC)
                            rows(g + 1)
                    if back:
                        ch.start((g - 1) * per_group)
                        wait(v, s_dmm, g - 1)
                        for c in range(GC):
                            n = (g - 1) * GC + c
                            col = (g - 1) * GC + c
                            v.tensor_scalar(oh_p[:, c], iota_p[:], digits[:, bass.ds(col, 1), 0], None, ALU.is_equal)
                            ins = v.tensor_scalar(oh_t[:, c], iota_p[:, 0:T], digits[:, bass.ds(col, 1), 1], None,
                                                  ALU.is_equal)
                        ins.then_inc(s_oh, 1)
                        for c in range(GC):
                            n = (g - 1) * GC + c
                            v.wait_ge(s_MR, n + 1)
                            wait(v, s_S, n - GC + 1)
                            v.tensor_scalar(same[:, c], bM[c % 2][:, 0:C], keys[:, c, 0:1], None, ALU.is_equal)
                            v.scalar_tensor_tensor(junk[:, c], bM[c % 2][:, 0:C], keys[:, c, 0:1], lower[:],
                                                   ALU.is_equal, ALU.mult, accum_out=before[:, c, 0:1])
                            v.scalar_tensor_tensor(junk2[:, c], bM[c % 2][:, C:2 * C], keys[:, c, 1:2], lower[:],
                                                   ALU.is_equal, ALU.mult, accum_out=before[:, c, 1:2])
                            v.tensor_scalar(junk3[:, c], bM[c % 2][:, C:2 * C], keys[:, c, 1:2], None, ALU.is_equal,
                                            ALU.add, accum_out=number[:, c:c + 1]).then_inc(s_M, 1)
                        for c in range(GC):
                            n = (g - 1) * GC + c
                            v.wait_ge(s_gt, n + 1)
                            wait(v, s_S, n - GC + 1)
                            v.tensor_tensor(msg[:, c, 0:D], gated[:, c], bO[c % 2][:, D:2 * D],
                                            ALU.mult).then_inc(s_msg, 1)
                        v.wait_ge(s_dmm, g)
                        wait(v, s_dg, g - 1)
                        v.tensor_tensor(degree[:], degree[:], bM[1][:, D:D + T], ALU.add).then_inc(s_dg, 1)
                        v.wait_ge(s_M, g * GC)
                        ch.link(v.tensor_scalar(later[:], before[:], 0.5, None, ALU.is_ge))
                        ch.link(v.scalar_tensor_tensor(away[:], keys[:], -1.0,
                                                       trash[:].unsqueeze(1).broadcast_to([P, GC, 2]),
                                                       ALU.mult, ALU.add))
                        ch.link(v.tensor_tensor(away[:], away[:], later[:], ALU.mult))
                        wait(v, s_cnt, 16 * GC * (g - 1))
                        wait(v, s_sums, 16 * GC * (g - 1))
                        ch.link(v.tensor_tensor(sidx[:], away[:], keys[:], ALU.add))
                        v.tensor_copy(number_out[:], number[:]).then_inc(s_fin, 1)
                    if front:
                        v.tensor_copy(keys[:], cells[:, bass.ds(g * GC, GC), :]).then_inc(s_ks, 1)

                v.memset(msg[:], 1.0).then_inc(s_one, 1)
                rows(0)
                v.wait_ge(s_one, 1)
                body(0, True, False)
                body(1, True, True)
                with v.Fori(2, G - 1) as g:
                    body(g, True, True)
                body(G - 1, True, True)
                body(G, False, True)

        ring = sb("ring", [P, B, TB, BW])
        buf = [sb(f"buf{i}", [P, T, D]) for i in range(3)]
        R = sb("R", [P, T, D])
        aggT = sb("aggT", [P, KD, BW])
        hst = sb("hst", [P, TB, D])
        hT = sb("hT", [P, TB, KD, P])
        stats = sb("stats", [P, TB, 6])
        mv = sb("mv", [P, TB, 2])
        rstd = sb("rstd", [P, TB])
        tmp = sb("tmp", [P, TB, D])
        w_l = sb("w_l", [P, KD, 2 * D])
        w_r = sb("w_r", [P, KD, D])
        bias_l = sb("bias_l", [P, 2, D])
        bias_r = sb("bias_r", [P, D])
        own, X1s, X2 = buf

        def flat(X, t):
            return X[:, bass.ds(t, 1), :].rearrange("p a c -> p (a c)")

        with ExitStack() as lc:
            tab = sb("tab", [P, TB, SW], c=lc)
            xs = sb("xs", [P, TB, D], c=lc)
            names1 = "in wt v v2 sq h cp tr xt rm r".split()
            N1 = {n: sem("n_" + n, lc) for n in names1}
            n_t = [sem(f"n_t{j}", lc) for j in range(TB)]
            bU, bV = psum[4:6], psum[6:8]
            block = lc.enter_context(nc.Block())

            def norm_loop(eng, body):
                body(0)
                with eng.Fori(1, B) as b:
                    body(b)

            @block.sync
            def _(sp):
                sp.dma_start(own[:], x_v).then_inc(N1["in"], 16)

                def body(b):
                    for j in range(TB):
                        n = b * TB + j
                        wait(sp, N1["h"], n - TB + 1)
                        sp.dma_start(tab[:, j], sums_v[:, bass.ds(n, 1), :].rearrange("p a w -> p (a w)")
                                     ).then_inc(n_t[j], 16)
                norm_loop(sp, body)

            @block.scalar
            def _(act):
                act.dma_start(w_l[:], gW.rearrange("(k p) n -> p k n", p=P)).then_inc(N1["wt"], 16)
                for q, row in enumerate((gb1, gb2)):
                    act.dma_start(bias_l[:, q], row.broadcast_to([P, D])).then_inc(N1["wt"], 16)
                act.wait_ge(N1["sq"], 1)
                act.activation(dinv[:], dinv[:], ACT.Sqrt).then_inc(N1["sq"], 1)

                def body(b):
                    for i in range(TB + 1):
                        n = b * TB + i
                        if i < TB:
                            act.wait_ge(N1["sq"], 2 * n + 3)
                            act.activation(rstd[:, i:i + 1], rstd[:, i:i + 1], ACT.Sqrt).then_inc(N1["sq"], 1)
                            act.wait_ge(N1["h"], n + 1)
                            act.copy(flat(X1s, n), xs[:, i]).then_inc(N1["cp"], 1)
                        if i >= 1:
                            act.wait_ge(N1["tr"], n)
                            wait(act, N1["rm"], n - TB)
                            act.copy(hT[:, i - 1], bV[(i - 1) % 2][:, 0:D].rearrange("p (k n) -> p k n", k=KD)
                                     ).then_inc(N1["xt"], 1)
                norm_loop(act, body)

            @block.tensor
            def _(pe):
                pe.wait_ge(N1["wt"], 48)

                def tr(n, i):
                    pe.wait_ge(N1["h"], n + 1)
                    wait(pe, N1["xt"], n if i == 0 else n - 1)
                    for k in range(KD):
                        mm = pe.transpose(bV[i % 2][:, k * P:(k + 1) * P], xs[:, i, k * P:(k + 1) * P], ident[:])
                    mm.then_inc(N1["tr"], 1)

                def rm(n, i):
                    pe.wait_ge(N1["xt"], n + 1)
                    wait(pe, N1["r"], n if i == 0 else n - 1)
                    for k in range(KD):
                        mm = pe.matmul(bU[i % 2][:, :], hT[:, i, k], w_l[:, k], start=(k == 0), stop=(k == KD - 1))
                    mm.then_inc(N1["rm"], 1)

                def body(b):
                    for i in range(TB + 1):
                        if i < TB:
                            tr(b * TB + i, i)
                        if i >= 1:
                            rm(b * TB + i - 1, i - 1)
                norm_loop(pe, body)

            @block.vector
            def _(v):
                ch = Chain(v, N1["v"])
                ch.link(v.tensor_scalar(dinv[:], degree[:], 1.0, None, ALU.add))
                v.tensor_scalar(dinv[:], dinv[:], 1.0, None, ALU.max).then_inc(N1["sq"], 1)
                v.wait_ge(N1["sq"], 2)
                ch.link(v.reciprocal(dinv[:], dinv[:]))
                ch.link(v.tensor_scalar(inv_dst[:], degree[:], 1.0, None, ALU.max))
                ch.link(v.reciprocal(inv_dst[:], inv_dst[:]))
                v.wait_ge(N1["in"], 16)
                v.wait_ge(N1["wt"], 48)
                first, per = ch.n, 7
                own_ch = Chain(v, N1["v2"])

                def body(b):
                    for i in range(TB + 2):
                        n = b * TB + i
                        if i < TB:
                            ch.start(first + n * per)
                            v.wait_ge(n_t[i], 16 * (b + 1))
                            one = inv_src[:, bass.ds(n, 1)]
                            wait(v, N1["cp"], n - TB + 1)
                            wait(v, N1["tr"], n - TB + 1)
                            ch.link(v.tensor_scalar(one, tab[:, i, D:D + 1], 1.0, None, ALU.max))
                            stand_alone(v, s_up)
                            ch.link(v.reciprocal(one, one))
                            ch.link(v.scalar_tensor_tensor(tmp[:, i], tab[:, i, 0:D], one, flat(own, n),
                                                           ALU.mult, ALU.add))
                            ch.link(v.bn_stats(stats[:, i], tmp[:, i]))
                            stand_alone(v, s_up)
                            ch.link(v.bn_aggr(mv[:, i], stats[:, i]))
                            v.tensor_scalar(rstd[:, i:i + 1], mv[:, i, 1:2], EPS, None, ALU.add).then_inc(N1["sq"], 1)
                            v.wait_ge(N1["sq"], 2 * n + 4)
                            stand_alone(v, s_up)
                            ch.link(v.reciprocal(rstd[:, i:i + 1], rstd[:, i:i + 1]))
                            ch.link(v.tensor_scalar(hst[:, i], tmp[:, i], mv[:, i, 0:1], rstd[:, i:i + 1],
                                                    ALU.subtract, ALU.mult))
                            v.tensor_scalar(xs[:, i], hst[:, i], dinv[:, bass.ds(n, 1)], None,
                                            ALU.mult).then_inc(N1["h"], 1)
                        if i >= 2:
                            m = n - 2
                            d = dinv[:, bass.ds(m, 1)]
                            U = bU[(i - 2) % 2]
                            v.wait_ge(N1["rm"], m + 1)
                            v.scalar_tensor_tensor(flat(R, m), U[:, 0:D], d, bias_l[:, 0], ALU.mult, ALU.add)
                            own_ch.start(m)
                            own_ch.link(v.scalar_tensor_tensor(tmp[:, i - 2], U[:, D:2 * D], d, bias_l[:, 1],
                                                           ALU.mult, ALU.add))
                            v.tensor_tensor(flat(own, m), tmp[:, i - 2], hst[:, i - 2], ALU.add).then_inc(N1["r"], 1)
                norm_loop(v, body)

        names = "wt gA pc g ev lin u tr xt rm r h cp sq st vc dn"
        S = {n: sem("a_" + n) for n in names.split()}
        s_A = [sem(f"a_A{i}") for i in range(B)]
        cnt = dict(passes=0, weights=0, vc=0, sq=0)

        def aggregate(kind, Xin, Xout, resid, w_left, w_right, b_right):
            k0 = cnt["passes"]
            b_off, t_off = k0 * B, k0 * T
            w_off = cnt["weights"]
            UW = 2 * D if kind == "gcn" else D
            norm = kind != "sage"
            banks, bU, bV = psum[0:4], psum[4:6], psum[6:8]
            per = real_per
            vc0, sq0 = cnt["vc"], cnt["sq"]
            n_w = 0
            with nc.Block() as block:
                @block.sync
                def _(sp):
                    def body(b):
                        for i in range(B):
                            if i < B - 1:
                                wait(sp, S["pc"], (b_off + b - 1) * (B - 1) + i + 1)
                            else:
                                wait(sp, S["g"], 4 * (b_off + b))
                            sp.dma_start(ring[:, i], counts_v[b, :, TB * i:TB * (i + 1), :]
                                         if isinstance(b, int) else
                                         counts_v[bass.ds(b, 1), :, TB * i:TB * (i + 1), :].rearrange("b p a c -> p (b a) c")
                                         ).then_inc(s_A[i], 16)
                    looped(sp, B, body)

                @block.tensor
                def _(pe):
                    pe.wait_ge(S["wt"], w_off + 16 * n_weights)

                    def tile_steps(b, i, what):
                        n = t_off + (b - 1) * TB + i
                        before = 1 if i == 0 else 2
                        if what == "lin":
                            wait(pe, S["h"], n - before + 1)
                            for k in range(KD):
                                mm = pe.matmul(bU[i % 2][:, 0:UW], aggT[:, k, i * P:(i + 1) * P], w_l[:, k, 0:UW],
                                               start=(k == 0), stop=(k == KD - 1))
                            mm.then_inc(S["lin"], 1)
                        elif what == "tr":
                            pe.wait_ge(S["h"], n + 1)
                            wait(pe, S["r"], n - before + 1)
                            for k in range(KD):
                                mm = pe.transpose(bV[i % 2][:, k * P:(k + 1) * P], hst[:, i, k * P:(k + 1) * P], ident[:])
                            mm.then_inc(S["tr"], 1)
                        else:
                            pe.wait_ge(S["xt"], n + 1)
                            for k in range(KD):
                                mm = pe.matmul(bV[i % 2][:, D:2 * D], hT[:, i, k], w_r[:, k],
                                               start=(k == 0), stop=(k == KD - 1))
                            mm.then_inc(S["rm"], 1)

                    def body(b, front, back):
                        if back:
                            pe.wait_ge(S["ev"], 4 * (b_off + b))
                        for i in range(B):
                            if front:
                                pe.wait_ge(s_A[i], 16 * (b_off + b + 1))
                                for a in range(TB):
                                    for q in range(4):
                                        if i == 0 and a == 0:
                                            wait(pe, S["ev"], 4 * (b_off + b - 1) + q + 1)
                                        h, w = q // 2, q % 2
                                        mm = pe.matmul(banks[q][:, 0:NW], Xin[:, TB * i + a, h * P:(h + 1) * P],
                                                       ring[:, i, a, w * NW:(w + 1) * NW],
                                                       start=(i == 0 and a == 0), stop=(i == B - 1 and a == TB - 1))
                                        if i == B - 1 and a == TB - 1:
                                            mm.then_inc(S["g"], 1)
                                        elif a == TB - 1 and q == 3:
                                            mm.then_inc(S["pc"], 1)
                            if back:
                                tile_steps(b, i, "lin")
                                if i >= 1:
                                    tile_steps(b, i - 1, "tr")
                                if i >= 2:
                                    tile_steps(b, i - 2, "rm")
                        if back:
                            tile_steps(b, B - 1, "tr")
                            tile_steps(b, B - 2, "rm")
                            tile_steps(b, B - 1, "rm")
                    body(0, True, False)
                    body(1, True, True)
                    with pe.Fori(2, B) as b:
                        body(b, True, True)
                    body(B, False, True)

                @block.scalar
                def _(act):
                    act.dma_start(w_l[:, :, 0:UW], w_left).then_inc(S["wt"], 16)
                    act.dma_start(w_r[:], w_right).then_inc(S["wt"], 16)
                    act.dma_start(bias_r[:], b_right.broadcast_to([P, D])).then_inc(S["wt"], 16)

                    def body(b, front, back):
                        if back:
                            for i in range(B + 1):
                                n = t_off + (b - 1) * TB + i
                                if i < B:
                                    if norm:
                                        act.wait_ge(S["sq"], sq0 + 2 * ((b - 1) * TB + i) + 1)
                                        act.activation(rstd[:, i:i + 1], rstd[:, i:i + 1], ACT.Sqrt).then_inc(S["sq"], 1)
                                    act.wait_ge(S["h"], n + 1)
                                    act.copy(Xout[:, bass.ds((b - 1) * TB + i, 1), :].rearrange("p a c -> p (a c)"),
                                             hst[:, i]).then_inc(S["cp"], 1)
                                if i >= 1:
                                    act.wait_ge(S["tr"], n)
                                    wait(act, S["rm"], n - TB)
                                    act.copy(hT[:, i - 1], bV[(i - 1) % 2][:, 0:D].rearrange("p (k n) -> p k n", k=KD)
                                             ).then_inc(S["xt"], 1)
                        if front:
                            wait(act, S["lin"], T * k0 + TB * b)
                            for q in range(4):
                                act.wait_ge(S["g"], 4 * (b_off + b) + q + 1)
                                h, w = q // 2, q % 2
                                act.copy(aggT[:, h, w * NW:(w + 1) * NW], banks[q][:, 0:NW]).then_inc(S["ev"], 1)
                    body(0, True, False)
                    body(1, True, True)
                    with act.Fori(2, B) as b:
                        body(b, True, True)
                    body(B, False, True)

                @block.vector
                def _(v):
                    ch = Chain(v, S["vc"])
                    v.wait_ge(S["wt"], w_off + 16 * n_weights)

                    def body(b):
                        for i in range(B + 2):
                            n = t_off + (b - 1) * TB + i
                            t = (b - 1) * TB + i
                            if i < B:
                                U = bU[i % 2]
                                ch.start(vc0 + t * per)
                                v.wait_ge(S["lin"], n + 1)
                                wait(v, S["tr"], n - TB + 1)
                                wait(v, S["cp"], n - TB + 1)
                                dst = hst[:, i]
                                if kind == "gcn":
                                    d = dinv[:, bass.ds(t, 1)]
                                    ch.link(v.scalar_tensor_tensor(tmp[:, i], U[:, 0:D], d, flat(R, t), ALU.mult, ALU.add))
                                    ch.link(v.scalar_tensor_tensor(dst, U[:, D:2 * D], d, flat(resid, t), ALU.mult, ALU.add))
                                    ch.link(v.scalar_tensor_tensor(tmp[:, i], tmp[:, i], 0.0, dst, ALU.max, ALU.add))
                                else:
                                    ch.link(v.scalar_tensor_tensor(tmp[:, i], U[:, 0:D], inv_dst[:, bass.ds(t, 1)],
                                                                   flat(R, t), ALU.mult, ALU.add))
                                    if kind == "last":
                                        ch.link(v.tensor_tensor(tmp[:, i], tmp[:, i], flat(resid, t), ALU.add))
                                if norm:
                                    ch.link(v.bn_stats(stats[:, i], tmp[:, i]))
                                    stand_alone(v, s_up)
                                    ch.link(v.bn_aggr(mv[:, i], stats[:, i]))
                                    v.tensor_scalar(rstd[:, i:i + 1], mv[:, i, 1:2], EPS, None, ALU.add).then_inc(S["sq"], 1)
                                    v.wait_ge(S["sq"], sq0 + 2 * t + 2)
                                    stand_alone(v, s_up)
                                    ch.link(v.reciprocal(rstd[:, i:i + 1], rstd[:, i:i + 1]))
                                    v.tensor_scalar(dst, tmp[:, i], mv[:, i, 0:1], rstd[:, i:i + 1],
                                                    ALU.subtract, ALU.mult).then_inc(S["h"], 1)
                                else:
                                    v.tensor_scalar(dst, tmp[:, i], 0.0, None, ALU.max).then_inc(S["h"], 1)
                                assert ch.n == real_per, (ch.n, real_per)
                            if i >= 2:
                                v.wait_ge(S["rm"], n - 1)
                                v.tensor_tensor(flat(R, t - 2), bV[(i - 2) % 2][:, D:2 * D], bias_r[:], ALU.add
                                                ).then_inc(S["r"], 1)
                    body(1)
                    with v.Fori(2, B) as b:
                        body(b)
                    body(B)
            cnt["passes"] += 1
            cnt["weights"] += 16 * n_weights
            cnt["vc"] += per * T
            cnt["sq"] += 2 * T if norm else 0

        def wview(W):
            return W.rearrange("(k p) n -> p k n", p=P)

        real_per, n_weights = 6, 3
        per_of = {"gcn": 6, "sage": 1, "last": 5}

        def run(kind, *args):
            nonlocal real_per, n_weights
            real_per, n_weights = per_of[kind], 3
            aggregate(kind, *args)

        run("gcn", X1s, X2, own, wview(gW), wview(Wr[0]), bl[0])
        run("sage", X2, own, None, wview(Wl[0]), wview(Wr[1]), bl[1])
        run("sage", own, X1s, None, wview(Wl[1]), wview(Wr[2]), bl[2])
        run("last", X1s, own, X2, wview(Wl[2]), wview(W3), b3)

        X3 = own
        with ExitStack() as fc:
            at0 = buf[1][:].rearrange("p a c -> p (a c)")[:, 0:T * P].rearrange("p (s n) -> p s n", s=T)
            at1 = buf[2][:].rearrange("p a c -> p (a c)")[:, 0:T * P].rearrange("p (s n) -> p s n", s=T)
            AT = [at0, at1]
            f = {n: sem("f_" + n, fc) for n in "tr ev mm vc sq h rd".split()}
            f_A = [sem(f"f_A{i}", fc) for i in range(B)]
            f_o = [sem(f"f_o{i}", fc) for i in range(B)]
            block = fc.enter_context(nc.Block())
            QN = (T + 3) // 4
            rows_v = counts_v.rearrange("b p a c -> p a b c")
            bU = psum[4:6]

            @block.sync
            def _(sp):
                def body(b):
                    for i in range(B):
                        n = b * TB + i
                        wait(sp, f["tr"], QN * (n - B + 1))
                        sp.dma_start(ring[:, i], rows_v[:, bass.ds(n, 1), :, :].rearrange("p a b c -> p (a b) c")
                                     ).then_inc(f_A[i], 16)
                    for i in range(B):
                        n = b * TB + i
                        sp.wait_ge(f["h"], n + 1)
                        sp.dma_start(out_v[:, bass.ds(n, 1), :].rearrange("p a c -> p (a c)"),
                                     hst[0:NODES // T, i]).then_inc(f_o[i], 16)
                looped(sp, B, body)
                for i in range(B):
                    sp.wait_ge(f_o[i], 16 * B)

            @block.tensor
            def _(pe):
                def mms(b, i, q):
                    n = b * TB + i
                    if q == 0:
                        pe.wait_ge(f["ev"], QN * (n + 1))
                        wait(pe, f["rd"], n if i == 0 else n - 1)
                    for s in range(4 * q, min(4 * q + 4, T)):
                        mm = pe.matmul(bU[i % 2][:, 0:D], AT[i % 2][:, s], R[:, s],
                                       start=(s == 0), stop=(s == T - 1))
                    if q == QN - 1:
                        mm.then_inc(f["mm"], 1)

                def trs(b, i, q):
                    n = b * TB + i
                    if q == 0:
                        pe.wait_ge(f_A[i], 16 * (b + 1))
                    wait(pe, f["ev"], QN * n + (q - 2 if q < 3 else q - 3))
                    for s in range(4 * q, min(4 * q + 4, T)):
                        j = s - 4 * q
                        mm = pe.transpose(psum[q % 4][:, j * P:(j + 1) * P], ring[:, i, s // TB, (s % TB) * P:(s % TB + 1) * P],
                                          ident[:])
                    mm.then_inc(f["tr"], 1)

                def body(b, first, last):
                    for i in range(B):
                        for q in range(QN):
                            trs(b, i, q)
                            if i >= 1:
                                mms(b, i - 1, q)
                    for q in range(QN):
                        mms(b, B - 1, q)
                looped(pe, B, lambda b: body(b, 0, 0))

            @block.scalar
            def _(act):
                def body(b):
                    for i in range(B):
                        n = b * TB + i
                        for q in range(QN):
                            w = min(4, T - 4 * q)
                            act.wait_ge(f["tr"], QN * n + q + 1)
                            if q == 0:
                                wait(act, f["mm"], n if i == 0 else n - 1)
                            act.copy(AT[i % 2][:, 4 * q:4 * q + w],
                                     psum[q % 4][:, 0:w * P].rearrange("p (s n) -> p s n", s=w)).then_inc(f["ev"], 1)
                        if i >= 1:
                            root(b, i - 1)
                    root(b, B - 1)

                def root(b, i):
                    n = b * TB + i
                    act.wait_ge(f["sq"], 2 * n + 1)
                    act.activation(rstd[:, i:i + 1], rstd[:, i:i + 1], ACT.Sqrt).then_inc(f["sq"], 1)
                looped(act, B, body)

            @block.vector
            def _(v):
                ch = Chain(v, f["vc"])

                def body(b):
                    for i in range(B):
                        n = b * TB + i
                        ch.start(n * 3)
                        v.wait_ge(f["mm"], n + 1)
                        v.scalar_tensor_tensor(tmp[:, i], bU[i % 2][:, 0:D], inv_src[:, bass.ds(n, 1)],
                                               X3[:, bass.ds(n, 1), :].rearrange("p a c -> p (a c)"),
                                               ALU.mult, ALU.add).then_inc(f["rd"], 1)
                        v.wait_ge(f["rd"], n + 1)
                        ch.link(v.bn_stats(stats[:, i], tmp[:, i]))
                        stand_alone(v, s_up)
                        ch.link(v.bn_aggr(mv[:, i], stats[:, i]))
                        v.tensor_scalar(rstd[:, i:i + 1], mv[:, i, 1:2], EPS, None, ALU.add).then_inc(f["sq"], 1)
                        v.wait_ge(f["sq"], 2 * n + 2)
                        stand_alone(v, s_up)
                        ch.link(v.reciprocal(rstd[:, i:i + 1], rstd[:, i:i + 1]))
                        wait(v, f_o[i], 16 * b)
                        v.tensor_scalar(hst[:, i], tmp[:, i], mv[:, i, 0:1], rstd[:, i:i + 1],
                                        ALU.subtract, ALU.mult).then_inc(f["h"], 1)
                looped(v, B, body)


def kernel(x, src, dst, edge_attr_128, **w):
    import numpy as np
    import concourse.bacc as bacc
    from concourse.bass_utils import run_bass_kernel_spmd

    def padded(a, shape):
        o = np.zeros(shape, a.dtype)
        o[tuple(slice(0, s) for s in a.shape)] = a
        return o

    def edges(a):
        o = np.full(EP, NP - 1, np.int32)
        o[:a.shape[0]] = np.asarray(a)
        return np.ascontiguousarray(o.reshape(G * GC, C).T)

    w = {k: np.asarray(v) for k, v in w.items()}
    xp = padded(np.asarray(x), (NP, D))
    W0 = padded(w["L0_gnn_W0"], (2 * D, H1))
    W1 = padded(w["L0_gnn_W1"], (H1, H2))
    W2b = np.concatenate([w["L0_gnn_W2"], w["L0_gnn_b2"][None]])
    arrays = {
        "xT": np.ascontiguousarray(xp.T),
        "x": xp,
        "src_col": edges(src),
        "dst_col": edges(dst),
        "edge_T": padded(np.asarray(edge_attr_128).T, (P, EP)),
        "W0": W0, "b0": padded(w["L0_gnn_b0"][None], (1, H1)),
        "W1": W1, "b1": np.ascontiguousarray(padded(w["L0_gnn_b1"], (H2,)).reshape(H2T, H2P).T),
        "W2b": W2b, "Wg": w["L0_gnn_Wg"],
        "gW": np.concatenate([w["L1_gnn_W1"], w["L1_gnn_W2"]], axis=1),
        "gb1": w["L1_gnn_b1"][None], "gb2": w["L1_gnn_b2"][None],
    }
    for i in (1, 2, 3):
        arrays[f"Wl{i}"] = np.ascontiguousarray(w[f"L2_gnn_W{i}l"].T)
        arrays[f"Wr{i}"] = np.ascontiguousarray(w[f"L2_gnn_W{i}r"].T)
        arrays[f"bl{i}"] = w[f"L2_gnn_b{i}l"][None]
    arrays["W3"], arrays["b3"] = w["L3_gnn_W"], w["L3_gnn_b"][None]
    nc = bacc.Bacc("TRN2", target_bir_lowering=False, num_devices=1)
    a = {n: nc.dram_tensor("in_" + n, v.shape, mybir.dt.from_np(v.dtype), kind="ExternalInput").ap()
         for n, v in arrays.items()}
    out = nc.dram_tensor("out", (NODES, D), F32, kind="ExternalOutput").ap()
    build(nc, a["xT"], a["x"], a["src_col"], a["dst_col"], a["edge_T"], a["W0"], a["b0"], a["W1"], a["b1"],
          a["W2b"], a["Wg"], a["gW"], a["gb1"], a["gb2"], [a["Wl1"], a["Wl2"], a["Wl3"]],
          [a["bl1"], a["bl2"], a["bl3"]], [a["Wr1"], a["Wr2"], a["Wr3"]], a["W3"], a["b3"], out)
    r = run_bass_kernel_spmd(nc, [{"in_" + n: v for n, v in arrays.items()}], core_ids=[0])
    return r.results[0]["out"]
```

```python
from contextlib import ExitStack

import concourse.bass as bass
from concourse import mybir

F32 = mybir.dt.float32
F32R = mybir.dt.float32r
BF16 = mybir.dt.bfloat16
I32 = mybir.dt.int32
ALU = mybir.AluOpType
ACT = mybir.ActivationFunctionType

P = 128
NODES = 3125
T = 25
NP = P * T
D = 256
KD = D // P
C = 128
GC = 4
G = 104
EP = G * GC * C
H1, H1T, H1P = 408, 4, 102
H2, H2T, H2P = 324, 3, 108
SW = D + 1
MW = D + 2
B = 5
TB = T // B
BW = TB * P
NW = BW // 2
HB = 2 * B
EXACT = 2048
OB = 16
ON = G * GC // OB
CELLS = NP * NP
EPS = 1e-5
ZW = 13 * SW


def wait(eng, sem, value):
    if not (isinstance(value, int) and value <= 0):
        eng.wait_ge(sem, value)


class Chain:

    def __init__(self, eng, sem):
        self.eng, self.sem, self.base, self.n = eng, sem, 0, 0

    def start(self, base):
        self.base, self.n = base, 0

    def link(self, ins):
        self.n += 1
        ins.then_inc(self.sem, 1)
        wait(self.eng, self.sem, self.base + self.n)


def stand_alone(eng, s_up):
    eng.sem_inc(s_up)


def looped(eng, n, body, head=1, tail=1):
    for i in range(head):
        body(i)
    with eng.Fori(head, n - tail) as i:
        body(i)
    for i in range(n - tail, n):
        body(i)


def layer_norm_stats(v, ch, src, stats, mv, std, eps_t):
    ch.link(v.bn_stats(stats, src))
    stand_alone(v, s_up)
    ch.link(v.bn_aggr(mv, stats))


def build(nc, xT, x, src_col, dst_col, edge_T, W0, b0, W1, b1, W2b, Wg, gW, gb1, gb2, Wl, bl, Wr, W3, b3, out):
    ctx = ExitStack()
    with ctx:
        def sb(name, shape, dt=F32, c=ctx):
            return c.enter_context(nc.sbuf_tensor(name, shape, dt))

        def sem(name, c=ctx):
            return c.enter_context(nc.semaphore(name))

        def dram(name, shape):
            return nc.dram_tensor(name, shape, F32)

        p_tab, q_tab = dram("p_tab", [NP, H1]), dram("q_tab", [NP, H1])
        sums = dram("sums", [NP + P, SW])
        counts = dram("counts", [CELLS + P, 1])
        sums_v = sums[0:NP, :].rearrange("(p a) w -> p a w", p=P)
        counts_v = counts[0:CELLS, :].rearrange("(b p a c) o -> b p a (c o)", b=HB, p=P, a=T)
        x_v = x.rearrange("(p a) c -> p a c", p=P)
        out_v = out.rearrange("(p a) c -> p a c", a=T)

        psum = [ctx.enter_context(nc.psum_tensor(f"bank{i}", [P, 512], F32)) for i in range(8)]

        s_up = sem("s_up")
        ident = sb("ident", [P, P])
        degree = sb("degree", [P, T])
        ones_row = sb("ones_row", [P, T])
        cnt_src = sb("cnt_src", [P, T])
        inv_src = sb("inv_src", [P, T])
        inv_dst = sb("inv_dst", [P, T])
        dinv = sb("dinv", [P, T])

        with ExitStack() as ec:
            def esb(name, shape, dt=F32):
                return sb(name, shape, dt, ec)

            def esem(name):
                return sem(name, ec)

            lower = esb("lower", [P, P])
            src_i = esb("src_i", [P, G * GC], I32)
            dst_i = esb("dst_i", [P, G * GC], I32)
            cells = esb("cells", [P, G * GC, 2])
            digits = esb("digits", [P, G * GC, 2])
            iota_p = esb("iota_p", [P, P])
            trash = esb("trash", [P, 2])
            w1, w1h, w1l = (esb(n, [H1P, H1T, H2]) for n in ("w1", "w1h", "w1l"))
            w2, w2h, w2l = (esb(n, [H2P, H2T, D]) for n in ("w2", "w2h", "w2l"))
            zeros = esb("zeros", [P, ZW])
            s_zd = esem("s_zd")
            n_zero = CELLS // (P * 3200)
            wg = esb("wg", [P, D])
            b1c = esb("b1c", [H2P, H2T])
            hidden1, hidden1h, hidden1l = (esb(n, [H1P, H1T, GC * C]) for n in ("hidden1", "hidden1h", "hidden1l"))
            hidden2, hidden2h, hidden2l = (esb(n, [H2P, H2T, GC * C]) for n in ("hidden2", "hidden2h", "hidden2l"))

            with ExitStack() as sc:
                def ssb(name, shape, dt=F32):
                    return sb(name, shape, dt, sc)

                def ssem(name):
                    return sem(name, sc)

                oh_p = ssb("oh_p", [P, 2, OB, P], BF16)
                oh_t = ssb("oh_t", [P, 2, OB, T], BF16)
                bf = ssb("bf", [P, G * GC])
                w0 = ssb("w0", [P, 2 * KD, H1])
                b0_b = ssb("b0_b", [P, H1])
                xt = ssb("xt", [P, TB, KD, P])
                p_out = ssb("p_out", [P, TB, H1])
                q_out = ssb("q_out", [P, TB, H1])
                sf = ssb("sf", [P, G * GC])
                df = ssb("df", [P, G * GC])
                qi = ssb("qi", [P, G * GC], I32)
                qf = ssb("qf", [P, G * GC])
                rf = ssb("rf", [P, G * GC])
                mf = ssb("mf", [P, G * GC])
                s_zero, s_w, s_idx = ssem("s_zero"), ssem("s_w"), ssem("s_idx")
                s_oh, s_deg, s_hi = ssem("s_oh"), ssem("s_deg"), ssem("s_hi")
                s_cg, s_cd = ssem("s_cg"), ssem("s_cd")
                s_pq, s_pe, s_qe = ssem("s_pq"), ssem("s_pe"), ssem("s_qe")
                s_xt = [ssem(f"s_xt{j}") for j in range(TB)]
                s_po = [ssem(f"s_po{j}") for j in range(TB)]
                s_qo = [ssem(f"s_qo{j}") for j in range(TB)]
                s_wl = ssem("s_wl")
                xT_v = xT.rearrange("(k p) n -> p k n", p=P)
                block = sc.enter_context(nc.Block())

                @block.sync
                def _(sp):
                    sp.dma_start(src_i[:], src_col).then_inc(s_idx, 16)
                    sp.dma_start(dst_i[:], dst_col).then_inc(s_idx, 16)
                    sp.dma_start(w0[:], W0.rearrange("(k p) n -> p k n", p=P)).then_inc(s_w, 16)
                    sp.dma_start(b0_b[:], b0.broadcast_to([P, H1])).then_inc(s_w, 16)

                    def body(b):
                        for j in range(TB):
                            n = b * TB + j
                            wait(sp, s_pq, n - TB + 1)
                            sp.dma_start(xt[:, j], xT_v[:, :, bass.ds(n * P, P)]).then_inc(s_xt[j], 16)
                        for j in range(TB):
                            n = b * TB + j
                            sp.wait_ge(s_pe, n + 1)
                            sp.dma_start(p_tab[bass.ds(n * P, P), :], p_out[:, j]).then_inc(s_po[j], 16)
                            sp.wait_ge(s_qe, n + 1)
                            sp.dma_start(q_tab[bass.ds(n * P, P), :], q_out[:, j]).then_inc(s_qo[j], 16)
                    looped(sp, B, body)
                    for j in range(TB):
                        sp.wait_ge(s_po[j], 16 * B)
                        sp.wait_ge(s_qo[j], 16 * B)

                @block.tensor
                def _(pe):
                    pe.wait_ge(s_w, 32)

                    def degrees(n, slot):
                        pe.wait_ge(s_oh, n + 1)
                        for c in range(OB):
                            mm = pe.matmul(psum[6][:, 0:T], oh_p[:, slot, c], oh_t[:, slot, c],
                                           start=(isinstance(n, int) and n == 0 and c == 0),
                                           stop=(isinstance(n, int) and n == ON - 1 and c == OB - 1),
                                           skip_group_check=True)
                        mm.then_inc(s_deg, 1)

                    def body(b):
                        for j in range(TB):
                            n = b * TB + j
                            pe.wait_ge(s_xt[j], 16 * (b + 1))
                            before = {0: n - 2, 1: n - 2, 2: n - 5, 3: n - 3, 4: n - 3}[j]
                            wait(pe, s_pe, before + 1)
                            wait(pe, s_qe, before + 1)
                            for half in range(2):
                                for k in range(KD):
                                    mm = pe.matmul(psum[2 * (j % 3) + half][:, 0:H1], xt[:, j, k], w0[:, 2 * half + k],
                                                   start=(k == 0), stop=(k == KD - 1))
                            mm.then_inc(s_pq, 1)
                    looped(pe, B, body)
                    degrees(0, 0)
                    degrees(1, 1)
                    with pe.Fori(1, ON // 2 - 1) as h:
                        degrees(2 * h, 0)
                        degrees(2 * h + 1, 1)
                    degrees(ON - 2, 0)
                    degrees(ON - 1, 1)

                @block.scalar
                def _(act):
                    act.wait_ge(s_zero, 1)
                    flat = counts[0:CELLS, :].rearrange("(m p c) o -> m p (c o)", p=P, c=3200)
                    for m in range(n_zero):
                        act.dma_start(flat[m], zeros[:, 0:3200]).then_inc(s_zd, 16)
                    act.dma_start(counts[CELLS:CELLS + P, :], zeros[:, 0:1]).then_inc(s_zd, 16)
                    for m in range(2):
                        act.dma_start(sums[m * 1664:(m + 1) * 1664, :].rearrange("(p a) w -> p (a w)", p=P),
                                      zeros[:]).then_inc(s_zd, 16)
                    act.dma_start(w1[:], W1.rearrange("(k p) n -> p k n", p=H1P)).then_inc(s_wl, 16)
                    act.dma_start(w2[:], W2b.rearrange("(k p) n -> p k n", p=H2P)).then_inc(s_wl, 16)
                    act.dma_start(wg[:], Wg).then_inc(s_wl, 16)
                    act.dma_start(b1c[:], b1).then_inc(s_wl, 16)

                    def body(b):
                        for j in range(TB):
                            n = b * TB + j
                            act.wait_ge(s_pq, n + 1)
                            wait(act, s_po[j], 16 * b)
                            act.copy(p_out[:, j], psum[2 * (j % 3)][:, 0:H1]).then_inc(s_pe, 1)
                    looped(act, B, body)
                    act.wait_ge(s_wl, 64)
                    act.copy(w1h[:].bitcast(F32R), w1[:]).then_inc(s_hi, 1)
                    act.copy(w2h[:].bitcast(F32R), w2[:]).then_inc(s_hi, 1)

                @block.gpsimd
                def _(pool):
                    pool.memset(ident[:], 0.0).then_inc(s_cg, 1)
                    pool.memset(lower[:], 1.0).then_inc(s_cg, 1)
                    pool.wait_ge(s_cg, 2)
                    pool.affine_select(out=ident[:], in_=ident[:], compare_op=ALU.not_equal, fill=1.0, base=0,
                                       pattern=[[-1, P]], channel_multiplier=1).then_inc(s_cg, 1)
                    pool.affine_select(out=lower[:], in_=lower[:], compare_op=ALU.is_gt, fill=0.0, base=0,
                                       pattern=[[-1, P]], channel_multiplier=1).then_inc(s_cg, 1)
                    pool.iota(iota_p[:], [[1, P]], base=0, channel_multiplier=0,
                              allow_small_or_imprecise_dtypes=True).then_inc(s_cg, 1)
                    pool.iota(trash[:, 0:1], [[0, 1]], base=NP, channel_multiplier=1,
                              allow_small_or_imprecise_dtypes=True).then_inc(s_cg, 1)
                    pool.iota(trash[:, 1:2], [[0, 1]], base=CELLS, channel_multiplier=1,
                              allow_small_or_imprecise_dtypes=True).then_inc(s_cg, 1)
                    pool.wait_ge(s_cg, 7)

                @block.vector
                def _(v):
                    v.memset(zeros[:], 0.0).then_inc(s_zero, 1)
                    ch = Chain(v, s_cd)
                    v.wait_ge(s_idx, 32)
                    ch.link(v.tensor_copy(df[:], dst_i[:]))
                    ch.link(v.tensor_copy(sf[:], src_i[:]))
                    ch.link(v.tensor_scalar(qi[:], df[:], 1.0 / T, -0.48, ALU.mult, ALU.add))
                    ch.link(v.tensor_copy(qf[:], qi[:]))
                    ch.link(v.scalar_tensor_tensor(rf[:], qf[:], -float(T), df[:], ALU.mult, ALU.add))
                    ch.link(v.tensor_scalar(mf[:], rf[:], float(T), None, ALU.is_ge))
                    ch.link(v.tensor_tensor(qf[:], qf[:], mf[:], ALU.add))
                    ch.link(v.scalar_tensor_tensor(rf[:], mf[:], -float(T), rf[:], ALU.mult, ALU.add))
                    ch.link(v.tensor_scalar(mf[:], rf[:], 0.0, None, ALU.is_lt))
                    ch.link(v.tensor_tensor(qf[:], qf[:], mf[:], ALU.subtract))
                    ch.link(v.scalar_tensor_tensor(rf[:], mf[:], float(T), rf[:], ALU.mult, ALU.add))
                    ch.link(v.tensor_copy(digits[:, :, 0], qf[:]))
                    ch.link(v.tensor_copy(digits[:, :, 1], rf[:]))
                    ch.link(v.scalar_tensor_tensor(qf[:], rf[:], float(P), qf[:], ALU.mult, ALU.add))
                    ch.link(v.tensor_scalar(bf[:], qf[:], float(NW), None, ALU.is_ge))
                    for k in range(2, HB):
                        ch.link(v.scalar_tensor_tensor(bf[:], qf[:], float(NW * k), bf[:], ALU.is_ge, ALU.add))
                    ch.link(v.scalar_tensor_tensor(qf[:], bf[:], float((NP - 1) * NW), qf[:], ALU.mult, ALU.add))
                    ch.link(v.scalar_tensor_tensor(qf[:], sf[:], float(NW), qf[:], ALU.mult, ALU.add))
                    ch.link(v.tensor_copy(cells[:, :, 0], sf[:]))
                    ch.link(v.tensor_copy(cells[:, :, 1], qf[:]))
                    v.wait_ge(s_w, 32)

                    v.wait_ge(s_cg, 7)

                    def one_hots(n, slot):
                        wait(v, s_deg, n - 1)
                        at = bass.ds(n * OB, OB)
                        v.tensor_tensor(oh_p[:, slot], iota_p[:].unsqueeze(1).broadcast_to([P, OB, P]),
                                        digits[:, at, 0:1].broadcast_to([P, OB, P]), ALU.is_equal)
                        v.tensor_tensor(oh_t[:, slot], iota_p[:, 0:T].unsqueeze(1).broadcast_to([P, OB, T]),
                                        digits[:, at, 1:2].broadcast_to([P, OB, T]), ALU.is_equal).then_inc(s_oh, 1)

                    def body(b):
                        for j in range(TB):
                            n = b * TB + j
                            v.wait_ge(s_pq, n + 1)
                            wait(v, s_qo[j], 16 * b)
                            v.tensor_tensor(q_out[:, j], psum[2 * (j % 3) + 1][:, 0:H1], b0_b[:],
                                            ALU.add).then_inc(s_qe, 1)
                    one_hots(0, 0)
                    one_hots(1, 1)
                    looped(v, B, body)
                    with v.Fori(1, ON // 2) as h:
                        one_hots(2 * h, 0)
                        one_hots(2 * h + 1, 1)
                    v.wait_ge(s_hi, 2)
                    v.tensor_tensor(w1l[:].bitcast(F32R), w1[:], w1h[:], ALU.subtract)
                    v.tensor_tensor(w2l[:].bitcast(F32R), w2[:], w2h[:], ALU.subtract)
                    v.wait_ge(s_deg, ON)
                    v.tensor_copy(degree[:], psum[6][:, 0:T])

            p_in = esb("p_in", [P, GC, H1])
            q_in = esb("q_in", [P, GC, H1])
            pre1 = esb("pre1", [P, GC, H1])
            gidx = esb("gidx", [P, 2, GC], I32)
            keys = esb("keys", [P, GC, 2])
            eT = esb("eT", [P, GC * C])
            same = esb("same", [P, GC, C])
            junk, junk2, junk3 = (esb(n, [P, GC, C]) for n in ("junk", "junk2", "junk3"))
            before = esb("before", [P, GC, 2])
            number = esb("number", [P, GC])
            later = esb("later", [P, GC, 2])
            away = esb("away", [P, GC, 2])
            gated = esb("gated", [P, GC, 2 * D])
            msg = esb("msg", [P, GC, D])
            msgh, msgl = esb("msgh", [P, GC, MW]), esb("msgl", [P, GC, MW])
            msum = esb("msum", [P, GC, SW])
            number_out = esb("number_out", [P, GC])
            sidx = esb("sidx", [P, GC, 2], I32)

            s_gp = [esem(f"s_gp{c}") for c in range(GC)]
            s_gq = [esem(f"s_gq{c}") for c in range(GC)]
            s_idxp = esem("s_idxp")
            s_idxq = esem("s_idxq")
            s_add = esem("s_add")
            s_T = esem("s_T")
            s_th1 = esem("s_th1")
            s_L1 = esem("s_L1")
            s_th2 = esem("s_th2")
            s_L2 = esem("s_L2")
            s_gt = esem("s_gt")
            s_msg = esem("s_msg")
            s_S = esem("s_S")
            s_sev = esem("s_sev")
            s_MR = esem("s_MR")
            s_M = esem("s_M")
            s_lo1 = esem("s_lo1")
            s_lo2 = esem("s_lo2")
            s_lom = esem("s_lom")
            s_him = esem("s_him")
            s_ks = esem("s_ks")
            s_fin = esem("s_fin")
            s_sums = esem("s_sums")
            s_cnt = esem("s_cnt")
            s_eT = esem("s_eT")
            s_vc = esem("s_vc")
            s_one = esem("s_one")
            bT, bH, bO, bM = psum[0:2], psum[2:4], psum[4:6], psum[6:8]
            bS = bO + bM
            blk = ec.enter_context(nc.Block())

            def edge_loop(eng, body):
                body(0, True, False)
                body(1, True, True)
                with eng.Fori(2, G) as g:
                    body(g, True, True)
                body(G, False, True)

            @blk.sync
            def _(sp):
                def body(g, front, back):
                    if front:
                        wait(sp, s_L2, g * GC)
                        sp.dma_start(eT[:], edge_T[:, bass.ds(g * (GC * C), GC * C)]).then_inc(s_eT, 16)
                edge_loop(sp, body)

            @blk.gpsimd
            def _(pool):
                def gather(c, tab, rows_in, which, done):
                    pool.indirect_dma_start(out=rows_in[:, c], out_offset=None, in_=tab[:],
                                            in_offset=bass.IndirectOffsetOnAxis(ap=gidx[:, which, c:c + 1], axis=0)
                                            ).then_inc(done[c], 16)

                def scatter(g, c):
                    n = g * GC + c
                    if c == 0:
                        pool.wait_ge(s_fin, g + 1)
                    wait(pool, s_cnt, 16 * n)
                    stand_alone(pool, s_up)
                    pool.indirect_dma_start(out=counts[:], in_=number_out[:, c:c + 1], in_offset=None,
                                            out_offset=bass.IndirectOffsetOnAxis(ap=sidx[:, c, 1:2], axis=0),
                                            compute_op=ALU.add).then_inc(s_cnt, 16)
                    pool.wait_ge(s_sev, n + 1)
                    wait(pool, s_sums, 16 * n)
                    stand_alone(pool, s_up)
                    pool.indirect_dma_start(out=sums[:], in_=msum[:, c], in_offset=None,
                                            out_offset=bass.IndirectOffsetOnAxis(ap=sidx[:, c, 0:1], axis=0),
                                            compute_op=ALU.add).then_inc(s_sums, 16)

                def body(g_in, g_out):
                    for c in range(GC):
                        if g_in is not None:
                            if c == 0:
                                pool.wait_ge(s_idxp, g_in + 1)
                            wait(pool, s_add, (g_in - 1) * GC + c + 1)
                            stand_alone(pool, s_up)
                            gather(c, p_tab, p_in, 0, s_gp)
                    for c in range(GC):
                        if g_out is not None:
                            scatter(g_out, c)
                        if g_in is not None:
                            if c == 0:
                                pool.wait_ge(s_idxq, g_in + 1)
                                stand_alone(pool, s_up)
                            gather(c, q_tab, q_in, 1, s_gq)
                body(0, None)
                body(1, None)
                body(2, None)
                pool.wait_ge(s_zd, 16 * (n_zero + 3))
                with pool.Fori(2, G - 1) as g:
                    body(g + 1, g - 2)
                for g in range(G - 3, G):
                    body(None, g)
                pool.wait_ge(s_sums, 16 * G * GC)
                pool.wait_ge(s_cnt, 16 * G * GC)

            @blk.tensor
            def _(pe):
                def transposes(g, c):
                    n = g * GC + c
                    pe.wait_ge(s_add, n + 1)
                    wait(pe, s_th1, n - 1)
                    for k in range(H1T):
                        mm = pe.transpose(bT[c % 2][0:H1P, k * C:(k + 1) * C],
                                          pre1[:, c, k * H1P:(k + 1) * H1P], ident[:])
                    mm.then_inc(s_T, 1)

                def split_product(out, lhs, rhs, first, last):
                    (lh, ll), (rh, rl) = lhs, rhs
                    pe.matmul(out, lh.bitcast(F32R), rh.bitcast(F32R), start=first, stop=False)
                    pe.matmul(out, lh.bitcast(F32R), rl.bitcast(F32R), start=False, stop=False)
                    return pe.matmul(out, ll.bitcast(F32R), rh.bitcast(F32R), start=False, stop=last)

                def first(g, m):
                    wait(pe, s_th2, H2T * g + m - 1 if m == 2 else H2T * g)
                    cols = slice(m * H2P, (m + 1) * H2P)
                    for k in range(H1T):
                        mm = split_product(bH[m % 2][0:H2P, :], (w1h[:, k, cols], w1l[:, k, cols]),
                                           (hidden1h[:, k], hidden1l[:, k]), k == 0, k == H1T - 1)
                    mm.then_inc(s_L1, 1)

                def second(g, c):
                    if c >= 2:
                        pe.wait_ge(s_gt, (g - 1) * GC + c - 1)
                    e = slice(c * C, (c + 1) * C)
                    for k in range(H2T):
                        split_product(bO[c % 2][:, 0:D], (hidden2h[:, k, e], hidden2l[:, k, e]),
                                      (w2h[:, k], w2l[:, k]), k == 0, k == H2T - 1)
                    pe.matmul(bO[c % 2][:, D:2 * D], eT[:, e], wg[:], start=True, stop=True).then_inc(s_L2, 1)

                def body(g, front, back):
                    if front:
                        transposes(g, 0)
                        transposes(g, 1)
                    if back:
                        pe.wait_ge(s_ks, g)
                        wait(pe, s_sev, (g - 1) * GC)
                        for c in range(GC):
                            for s in range(2):
                                at = (c % 2) * 2 * C + s * C
                                mm = pe.transpose(bM[c // 2][:, at:at + C],
                                                  keys[:, c, s:s + 1].broadcast_to([P, P]), ident[:])
                            mm.then_inc(s_MR, 1)
                    if front:
                        transposes(g, 2)
                    if back:
                        pe.wait_ge(s_th2, H2T * g)
                        pe.wait_ge(s_lo2, H2T * g)
                        pe.wait_ge(s_eT, 16 * g)
                        second(g, 0)
                    if front:
                        transposes(g, 3)
                    if back:
                        for c in range(1, GC):
                            second(g, c)
                    if front:
                        pe.wait_ge(s_th1, (g + 1) * GC)
                        pe.wait_ge(s_lo1, (g + 1) * GC)
                        for m in range(H2T - 1):
                            first(g, m)
                    if back:
                        pe.wait_ge(s_M, g * GC)
                        pe.wait_ge(s_him, g * GC)
                        pe.wait_ge(s_lom, g * GC)
                        pe.wait_ge(s_gt, g * GC)
                        for c in range(GC):
                            eq = same[:, c].bitcast(F32R)
                            pe.matmul(bS[c][:, 0:MW], eq, msgh[:, c].bitcast(F32R), start=True, stop=False)
                            pe.matmul(bS[c][:, 0:MW], eq, msgl[:, c].bitcast(F32R), start=False,
                                      stop=True).then_inc(s_S, 1)
                    if front:
                        first(g, H2T - 1)
                edge_loop(pe, body)

            @blk.scalar
            def _(act):
                act.wait_ge(s_one, 4)

                def body(g, front, back):
                    if front:
                        wait(act, s_L1, H2T * g)
                        wait(act, s_lo1, GC * g)
                        for c in range(GC):
                            n = g * GC + c
                            e = slice(c * C, (c + 1) * C)
                            act.wait_ge(s_T, n + 1)
                            src = bT[c % 2][0:H1P, :].rearrange("p (k e) -> p k e", k=H1T)
                            act.activation(hidden1[:, :, e], src, ACT.Tanh)
                            act.activation(hidden1h[:, :, e].bitcast(F32R), src, ACT.Tanh).then_inc(s_th1, 1)
                    if back:
                        for c in range(GC):
                            n = (g - 1) * GC + c
                            act.wait_ge(s_L2, n + 1)
                            wait(act, s_msg, n - GC + 1)
                            act.copy(gated[:, c], bO[c % 2][:, :]).then_inc(s_gt, 1)
                        wait(act, s_S, GC * (g - 1))
                        wait(act, s_lom, GC * (g - 1))
                        for c in range(GC):
                            act.wait_ge(s_msg, (g - 1) * GC + c + 1)
                            act.copy(msgh[:, c, 0:D].bitcast(F32R), msg[:, c]).then_inc(s_him, 1)
                    def second_tanh(m):
                        rows = H2P - 1 if m == H2T - 1 else H2P
                        act.wait_ge(s_L1, H2T * g + m + 1)
                        act.activation(hidden2[0:rows, m], bH[m % 2][0:rows, :], ACT.Tanh, bias=b1c[0:rows, m:m + 1])
                        act.activation(hidden2h[0:rows, m].bitcast(F32R), bH[m % 2][0:rows, :], ACT.Tanh,
                                       bias=b1c[0:rows, m:m + 1]).then_inc(s_th2, 1)
                    if front:
                        wait(act, s_L2, GC * g)
                        wait(act, s_lo2, H2T * g)
                        for m in range(H2T - 1):
                            second_tanh(m)
                    if back:
                        for c in range(GC):
                            n = (g - 1) * GC + c
                            act.wait_ge(s_S, n + 1)
                            wait(act, s_sums, 16 * (n - GC + 1))
                            act.copy(msum[:, c], bS[c][:, 0:SW]).then_inc(s_sev, 1)
                    if front:
                        second_tanh(H2T - 1)
                edge_loop(act, body)

            @blk.vector
            def _(v):
                ch = Chain(v, s_vc)
                per_group = 4

                def sender_rows(g):
                    v.tensor_copy(gidx[:, 0], src_i[:, bass.ds(g * GC, GC)]).then_inc(s_idxp, 1)

                def receiver_rows(g):
                    v.tensor_copy(gidx[:, 1], dst_i[:, bass.ds(g * GC, GC)]).then_inc(s_idxq, 1)

                def adds(g, chunks, more=True):
                    for c in chunks:
                        if c == 0:
                            for i in range(GC):
                                v.wait_ge(s_gp[i], 16 * (g + 1))
                            if more:
                                sender_rows(g + 1)
                        v.wait_ge(s_gq[c], 16 * (g + 1))
                        wait(v, s_T, (g - 1) * GC + c + 1)
                        if c == GC - 1 and more:
                            receiver_rows(g + 1)
                        v.tensor_tensor(pre1[:, c], p_in[:, c], q_in[:, c], ALU.add).then_inc(s_add, 1)

                def compare(g, c):
                    n = (g - 1) * GC + c
                    at = (c % 2) * 2 * C
                    row_s, row_k = bM[c // 2][:, at:at + C], bM[c // 2][:, at + C:at + 2 * C]
                    v.wait_ge(s_MR, (g - 1) * GC + 2 * (c // 2) + 2)
                    wait(v, s_S, n - GC + 1)
                    v.tensor_scalar(same[:, c].bitcast(F32R), row_s, keys[:, c, 0:1], None, ALU.is_equal)
                    v.scalar_tensor_tensor(junk[:, c], row_s, keys[:, c, 0:1], lower[:],
                                           ALU.is_equal, ALU.mult, accum_out=before[:, c, 0:1])
                    v.scalar_tensor_tensor(junk2[:, c], row_k, keys[:, c, 1:2], lower[:],
                                           ALU.is_equal, ALU.mult, accum_out=before[:, c, 1:2])
                    v.tensor_scalar(junk3[:, c], row_k, keys[:, c, 1:2], None, ALU.is_equal,
                                    ALU.add, accum_out=number[:, c:c + 1]).then_inc(s_M, 1)

                def body(g, front, back, more=2):
                    def cells_out():
                        if back:
                            wait(v, s_cnt, 16 * GC * (g - 1))
                            wait(v, s_sums, 16 * GC * (g - 1))
                            ch.link(v.tensor_tensor(sidx[:], away[:], keys[:], ALU.add))
                            v.tensor_copy(number_out[:], number[:]).then_inc(s_fin, 1)
                        if front:
                            v.tensor_copy(keys[:], cells[:, bass.ds(g * GC, GC), :]).then_inc(s_ks, 1)
                    for c in range(GC):
                        if back:
                            compare(g, c)
                        if front:
                            n = g * GC + c
                            e = slice(c * C, (c + 1) * C)
                            v.wait_ge(s_th1, n + 1)
                            if c == 0:
                                wait(v, s_L1, H2T * g)
                            v.tensor_tensor(hidden1l[:, :, e].bitcast(F32R), hidden1[:, :, e], hidden1h[:, :, e],
                                            ALU.subtract).then_inc(s_lo1, 1)
                    if back:
                        ch.start((g - 1) * per_group)
                        for c in range(GC):
                            n = (g - 1) * GC + c
                            v.wait_ge(s_gt, n + 1)
                            wait(v, s_him, n - GC + 1)
                            wait(v, s_lom, n - GC + 1)
                            v.tensor_tensor(msg[:, c], gated[:, c, 0:D], gated[:, c, D:2 * D],
                                            ALU.mult).then_inc(s_msg, 1)
                        for c in range(GC):
                            n = (g - 1) * GC + c
                            v.wait_ge(s_him, n + 1)
                            v.tensor_tensor(msgl[:, c, 0:D].bitcast(F32R), msg[:, c], msgh[:, c, 0:D],
                                            ALU.subtract).then_inc(s_lom, 1)
                        v.wait_ge(s_M, g * GC)
                        ch.link(v.tensor_scalar(later[:], before[:], 0.5, None, ALU.is_ge))
                        ch.link(v.scalar_tensor_tensor(away[:], keys[:], -1.0,
                                                       trash[:].unsqueeze(1).broadcast_to([P, GC, 2]),
                                                       ALU.mult, ALU.add))
                        ch.link(v.tensor_tensor(away[:], away[:], later[:], ALU.mult))
                    if front:
                        for m in range(H2T):
                            if m == H2T - 1:
                                cells_out()
                            if more > 0:
                                adds(g + 1, ([0, 1], [2, 3], [])[m], more > 1)
                            rows_m = H2P - 1 if m == H2T - 1 else H2P
                            v.wait_ge(s_th2, H2T * g + m + 1)
                            if m == 0:
                                wait(v, s_L2, GC * g)
                            v.tensor_tensor(hidden2l[0:rows_m, m].bitcast(F32R), hidden2[0:rows_m, m],
                                            hidden2h[0:rows_m, m], ALU.subtract).then_inc(s_lo2, 1)
                    else:
                        cells_out()

                v.memset(msgh[:], 1.0).then_inc(s_one, 1)
                v.memset(msgl[:], 0.0).then_inc(s_one, 1)
                v.memset(hidden2h[:], 1.0).then_inc(s_one, 1)
                v.memset(hidden2l[:], 0.0).then_inc(s_one, 1)
                sender_rows(0)
                receiver_rows(0)
                adds(0, range(GC))
                v.wait_ge(s_one, 4)
                body(0, True, False)
                body(1, True, True)
                with v.Fori(2, G - 2) as g:
                    body(g, True, True)
                body(G - 2, True, True, 1)
                body(G - 1, True, True, 0)
                body(G, False, True, 0)

        high = [sb(f"high{i}", [P, T, D]) for i in range(2)]
        low = [sb(f"low{i}", [P, T, D]) for i in range(2)]
        own = sb("own", [P, T, D])
        R = sb("R", [P, T, D])
        hst = sb("hst", [P, TB, D])
        hT = sb("hT", [P, 2, KD, P])
        stats = sb("stats", [P, TB, 6])
        mv = sb("mv", [P, TB, 2])
        rstd = sb("rstd", [P, TB])
        w_l = sb("w_l", [P, KD, 2 * D])
        w_r = sb("w_r", [P, KD, D])
        bias_r = sb("bias_r", [P, D])
        many = sb("many", [1, 1], I32)

        def flat(X, t):
            return X[:, bass.ds(t, 1), :].rearrange("p a c -> p (a c)")

        with ExitStack() as lc:
            tab = sb("tab", [P, TB, SW], c=lc)
            xs = sb("xs", [P, TB, D], c=lc)
            tmp = sb("tmp", [P, TB, D], c=lc)
            bias_l = sb("bias_l", [P, 2, D], c=lc)
            most = sb("most", [P, 4], c=lc)
            names1 = "in wt v v2 sq h cp tr xt rm r mx mt".split()
            N1 = {n: sem("n_" + n, lc) for n in names1}
            n_t = [sem(f"n_t{j}", lc) for j in range(TB)]
            bU, bV = psum[4:6], psum[6:8]
            block = lc.enter_context(nc.Block())

            def norm_loop(eng, body):
                body(0)
                with eng.Fori(1, B) as b:
                    body(b)

            @block.sync
            def _(sp):
                sp.dma_start(own[:], x_v).then_inc(N1["in"], 16)

                def body(b):
                    for j in range(TB):
                        n = b * TB + j
                        wait(sp, N1["h"], n - TB + 1)
                        sp.dma_start(tab[:, j], sums_v[:, bass.ds(n, 1), :].rearrange("p a w -> p (a w)")
                                     ).then_inc(n_t[j], 16)
                norm_loop(sp, body)

            @block.scalar
            def _(act):
                act.dma_start(w_l[:], gW.rearrange("(k p) n -> p k n", p=P)).then_inc(N1["wt"], 16)
                for q, row in enumerate((gb1, gb2)):
                    act.dma_start(bias_l[:, q], row.broadcast_to([P, D])).then_inc(N1["wt"], 16)
                act.wait_ge(N1["sq"], 1)
                act.activation(dinv[:], dinv[:], ACT.Sqrt).then_inc(N1["sq"], 1)

                def body(b):
                    for i in range(TB + 1):
                        n = b * TB + i
                        if i < TB:
                            act.wait_ge(N1["sq"], 2 * n + 3)
                            act.activation(rstd[:, i:i + 1], rstd[:, i:i + 1], ACT.Sqrt).then_inc(N1["sq"], 1)
                            act.wait_ge(N1["h"], n + 1)
                            act.copy(flat(high[0], n).bitcast(F32R), xs[:, i]).then_inc(N1["cp"], 1)
                        if i >= 1:
                            act.wait_ge(N1["tr"], n)
                            wait(act, N1["rm"], n - 1 if i == 1 else n - 2)
                            act.copy(hT[:, (i - 1) % 2], bV[(i - 1) % 2][:, 0:D].rearrange("p (k n) -> p k n", k=KD)
                                     ).then_inc(N1["xt"], 1)
                norm_loop(act, body)

            @block.tensor
            def _(pe):
                pe.wait_ge(N1["wt"], 48)
                pe.wait_ge(N1["mx"], 1)
                pe.transpose(psum[0][0:1, 0:P], most[:, 0:1], ident[:]).then_inc(N1["mt"], 1)

                def tr(n, i):
                    pe.wait_ge(N1["h"], n + 1)
                    wait(pe, N1["xt"], n if i == 0 else n - 1)
                    for k in range(KD):
                        mm = pe.transpose(bV[i % 2][:, k * P:(k + 1) * P], xs[:, i, k * P:(k + 1) * P], ident[:])
                    mm.then_inc(N1["tr"], 1)

                def rm(n, i):
                    pe.wait_ge(N1["xt"], n + 1)
                    wait(pe, N1["r"], n if i == 0 else n - 1)
                    for k in range(KD):
                        mm = pe.matmul(bU[i % 2][:, :], hT[:, i % 2, k], w_l[:, k], start=(k == 0), stop=(k == KD - 1))
                    mm.then_inc(N1["rm"], 1)

                def body(b):
                    for i in range(TB + 1):
                        if i < TB:
                            tr(b * TB + i, i)
                        if i >= 1:
                            rm(b * TB + i - 1, i - 1)
                norm_loop(pe, body)

            @block.vector
            def _(v):
                ch = Chain(v, N1["v"])
                ch.link(v.tensor_scalar(dinv[:], degree[:], 1.0, None, ALU.add))
                v.tensor_scalar(dinv[:], dinv[:], 1.0, None, ALU.max).then_inc(N1["sq"], 1)
                v.wait_ge(N1["sq"], 2)
                ch.link(v.reciprocal(dinv[:], dinv[:]))
                ch.link(v.tensor_scalar(inv_dst[:], degree[:], 1.0, None, ALU.max))
                ch.link(v.reciprocal(inv_dst[:], inv_dst[:]))
                v.tensor_reduce(most[:, 0:1], degree[:], mybir.AxisListType.X, ALU.max).then_inc(N1["mx"], 1)
                v.wait_ge(N1["mt"], 1)
                ch.link(v.tensor_reduce(most[0:1, 1:2], psum[0][0:1, 0:P], mybir.AxisListType.X, ALU.max))
                ch.link(v.tensor_scalar(most[0:1, 2:3], most[0:1, 1:2], float(EXACT), None, ALU.is_gt))
                ch.link(v.tensor_copy(many[:], most[0:1, 2:3]))
                v.wait_ge(N1["in"], 16)
                v.wait_ge(N1["wt"], 48)
                first, per = ch.n, 7
                own_ch = Chain(v, N1["v2"])

                def body(b):
                    for i in range(TB + 2):
                        n = b * TB + i
                        if i < TB:
                            ch.start(first + n * per)
                            v.wait_ge(n_t[i], 16 * (b + 1))
                            one = inv_src[:, bass.ds(n, 1)]
                            wait(v, N1["cp"], n - TB + 1)
                            wait(v, N1["tr"], n - TB + 1)
                            ch.link(v.tensor_scalar(one, tab[:, i, D:D + 1], 1.0, None, ALU.max))
                            stand_alone(v, s_up)
                            ch.link(v.reciprocal(one, one))
                            ch.link(v.scalar_tensor_tensor(tmp[:, i], tab[:, i, 0:D], one, flat(own, n),
                                                           ALU.mult, ALU.add))
                            ch.link(v.bn_stats(stats[:, i], tmp[:, i]))
                            stand_alone(v, s_up)
                            ch.link(v.bn_aggr(mv[:, i], stats[:, i]))
                            v.tensor_scalar(rstd[:, i:i + 1], mv[:, i, 1:2], EPS, None, ALU.add).then_inc(N1["sq"], 1)
                            v.wait_ge(N1["sq"], 2 * n + 4)
                            stand_alone(v, s_up)
                            ch.link(v.reciprocal(rstd[:, i:i + 1], rstd[:, i:i + 1]))
                            ch.link(v.tensor_scalar(hst[:, i], tmp[:, i], mv[:, i, 0:1], rstd[:, i:i + 1],
                                                    ALU.subtract, ALU.mult))
                            v.tensor_scalar(xs[:, i], hst[:, i], dinv[:, bass.ds(n, 1)], None,
                                            ALU.mult).then_inc(N1["h"], 1)
                        if i >= 2:
                            m = n - 2
                            d = dinv[:, bass.ds(m, 1)]
                            U = bU[(i - 2) % 2]
                            v.wait_ge(N1["rm"], m + 1)
                            v.scalar_tensor_tensor(flat(R, m), U[:, 0:D], d, bias_l[:, 0], ALU.mult, ALU.add)
                            own_ch.start(m)
                            own_ch.link(v.scalar_tensor_tensor(tmp[:, i - 2], U[:, D:2 * D], d, bias_l[:, 1],
                                                           ALU.mult, ALU.add))
                            v.tensor_tensor(flat(own, m), tmp[:, i - 2], hst[:, i - 2], ALU.add)
                            v.wait_ge(N1["cp"], m + 1)
                            v.tensor_tensor(flat(low[0], m).bitcast(F32R), xs[:, i - 2], flat(high[0], m),
                                            ALU.subtract).then_inc(N1["r"], 1)
                norm_loop(v, body)

        ring = sb("ring", [P, B, TB, NW])
        S = {n: sem("a_" + n) for n in "wt pc g ev lin u tr xt rm r h cp sq vc v2 vt".split()}
        s_A = [sem(f"a_A{i}") for i in range(B)]
        wview = lambda W: W.rearrange("(k p) n -> p k n", p=P)

        with ExitStack() as ac:
            aggT = sb("aggT", [P, KD, BW], c=ac)
            tmp = sb("tmp1", [P, D], c=ac)

            def aggregate(k, kind, src, dst, w_left, w_right, b_right):
                b_off, t_off = k * B, k * T
                UW = 2 * D if kind == "gcn" else D
                norm = kind != "sage"
                links = {"gcn": 6, "sage": 1, "last": 5}[kind]
                links_off = sum(T * n for n in (6, 1, 1)[:k])
                roots_off = 2 * T * min(k, 1)
                Xh, Xl, Yh, Yl = high[src], low[src], high[dst], low[dst]
                banks, bU, bV = psum[0:4], psum[4:6], psum[6:8]
                with nc.Block() as block:
                    @block.sync
                    def _(sp):
                        def body(hb):
                            m = HB * k + hb
                            for i in range(B):
                                if i < B - 1:
                                    wait(sp, S["pc"], (m - 1) * (B - 1) + i + 1)
                                else:
                                    wait(sp, S["g"], 2 * m)
                                sp.dma_start(ring[:, i], counts_v[bass.ds(hb, 1), :, TB * i:TB * (i + 1), :]
                                             .rearrange("b p a c -> p (b a) c")).then_inc(s_A[i], 16)
                        looped(sp, HB, body)

                    @block.tensor
                    def _(pe):
                        pe.wait_ge(S["wt"], 48 * (k + 1))

                        def tile_steps(b, i, what):
                            n = t_off + (b - 1) * TB + i
                            before = 1 if i == 0 else 2
                            if what == "lin":
                                wait(pe, S["h"], n - before + 1)
                                for h in range(KD):
                                    mm = pe.matmul(bU[i % 2][:, 0:UW], aggT[:, h, i * P:(i + 1) * P],
                                                   w_l[:, h, 0:UW], start=(h == 0), stop=(h == KD - 1))
                                mm.then_inc(S["lin"], 1)
                            elif what == "tr":
                                pe.wait_ge(S["h"], n + 1)
                                wait(pe, S["r"], n - before + 1)
                                for h in range(KD):
                                    mm = pe.transpose(bV[i % 2][:, h * P:(h + 1) * P],
                                                      hst[:, i, h * P:(h + 1) * P], ident[:])
                                mm.then_inc(S["tr"], 1)
                            else:
                                pe.wait_ge(S["xt"], n + 1)
                                for h in range(KD):
                                    mm = pe.matmul(bV[i % 2][:, D:2 * D], hT[:, i % 2, h], w_r[:, h],
                                                   start=(h == 0), stop=(h == KD - 1))
                                mm.then_inc(S["rm"], 1)

                        def sums(b, w, i, dt):
                            pe.wait_ge(s_A[i], 16 * (2 * (b_off + b) + w + 1))
                            for a in range(TB):
                                for h in range(KD):
                                    q = 2 * w + h
                                    first, last = i == 0 and a == 0, i == B - 1 and a == TB - 1
                                    if first:
                                        wait(pe, S["ev"], 4 * (b_off + b - 1) + q + 1)
                                    for part in (Xh, Xl):
                                        mm = pe.matmul(banks[q][:, 0:NW],
                                                       part[:, TB * i + a, h * P:(h + 1) * P].bitcast(dt),
                                                       ring[:, i, a].bitcast(dt),
                                                       start=first and part is Xh, stop=last and part is Xl)
                                    if last:
                                        mm.then_inc(S["g"], 1)
                            if i < B - 1:
                                mm.then_inc(S["pc"], 1)

                        def body(b, front, back, dt):
                            if back:
                                pe.wait_ge(S["ev"], 4 * (b_off + b))
                            for i in range(B):
                                if front:
                                    sums(b, 0, i, dt)
                                if back:
                                    tile_steps(b, i, "lin")
                                    if i >= 1:
                                        tile_steps(b, i - 1, "tr")
                                    if i >= 2:
                                        tile_steps(b, i - 2, "rm")
                            for i in range(B):
                                if front:
                                    sums(b, 1, i, dt)
                                if back and i == 0:
                                    tile_steps(b, B - 1, "tr")
                                    tile_steps(b, B - 2, "rm")
                                if back and i == 1:
                                    tile_steps(b, B - 1, "rm")

                        def blocks(dt):
                            body(0, True, False, dt)
                            body(1, True, True, dt)
                            with pe.Fori(2, B) as b:
                                body(b, True, True, dt)
                            body(B, False, True, dt)

                        exact = pe.value_load(many[0:1, 0:1], min_val=0, max_val=1)
                        with pe.If(exact < 1):
                            blocks(F32R)
                        with pe.Else():
                            blocks(F32)

                    @block.scalar
                    def _(act):
                        act.dma_start(w_l[:, :, 0:UW], w_left).then_inc(S["wt"], 16)
                        act.dma_start(w_r[:], w_right).then_inc(S["wt"], 16)
                        act.dma_start(bias_r[:], b_right.broadcast_to([P, D])).then_inc(S["wt"], 16)

                        def body(b, front, back):
                            if back:
                                for i in range(B + 1):
                                    n = t_off + (b - 1) * TB + i
                                    t = (b - 1) * TB + i
                                    if i < B:
                                        if norm:
                                            act.wait_ge(S["sq"], roots_off + 2 * t + 1)
                                            act.activation(rstd[:, i:i + 1], rstd[:, i:i + 1], ACT.Sqrt
                                                           ).then_inc(S["sq"], 1)
                                        act.wait_ge(S["h"], n + 1)
                                        if kind == "gcn":
                                            act.copy(flat(own, t), hst[:, i])
                                        if kind == "last":
                                            act.copy(flat(own, t), hst[:, i]).then_inc(S["cp"], 1)
                                        else:
                                            act.copy(flat(Yh, t).bitcast(F32R), hst[:, i]).then_inc(S["cp"], 1)
                                    if i >= 1:
                                        act.wait_ge(S["tr"], n)
                                        wait(act, S["rm"], n - 1 if i == 1 else n - 2)
                                        act.copy(hT[:, (i - 1) % 2],
                                                 bV[(i - 1) % 2][:, 0:D].rearrange("p (k n) -> p k n", k=KD)
                                                 ).then_inc(S["xt"], 1)
                            if front:
                                wait(act, S["lin"], t_off + TB * b)
                                for q in range(4):
                                    act.wait_ge(S["g"], 4 * (b_off + b) + q + 1)
                                    w, h = q // 2, q % 2
                                    act.copy(aggT[:, h, w * NW:(w + 1) * NW], banks[q][:, 0:NW]).then_inc(S["ev"], 1)
                        body(0, True, False)
                        body(1, True, True)
                        with act.Fori(2, B) as b:
                            body(b, True, True)
                        body(B, False, True)

                    @block.vector
                    def _(v):
                        ch, rch = Chain(v, S["vc"]), Chain(v, S["v2"])
                        v.wait_ge(S["wt"], 48 * (k + 1))

                        def body(b):
                            for i in range(B + 2):
                                n = t_off + (b - 1) * TB + i
                                t = (b - 1) * TB + i
                                if i < B:
                                    U, out_t = bU[i % 2], hst[:, i]
                                    ch.start(links_off + t * links)
                                    v.wait_ge(S["lin"], n + 1)
                                    wait(v, S["tr"], n - TB + 1)
                                    wait(v, S["cp"], n - TB + 1)
                                    wait(v, S["vt"], n - TB + 1)
                                    wait(v, S["h"], n)
                                    if kind == "gcn":
                                        d = dinv[:, bass.ds(t, 1)]
                                        ch.link(v.scalar_tensor_tensor(tmp[:], U[:, 0:D], d, flat(R, t),
                                                                       ALU.mult, ALU.add))
                                        ch.link(v.scalar_tensor_tensor(out_t, U[:, D:2 * D], d, flat(own, t),
                                                                       ALU.mult, ALU.add))
                                        ch.link(v.scalar_tensor_tensor(tmp[:], tmp[:], 0.0, out_t, ALU.max, ALU.add))
                                    else:
                                        ch.link(v.scalar_tensor_tensor(tmp[:], U[:, 0:D], inv_dst[:, bass.ds(t, 1)],
                                                                       flat(R, t), ALU.mult, ALU.add))
                                        if kind == "last":
                                            ch.link(v.tensor_tensor(tmp[:], tmp[:], flat(own, t), ALU.add))
                                    if norm:
                                        ch.link(v.bn_stats(stats[:, i], tmp[:]))
                                        stand_alone(v, s_up)
                                        ch.link(v.bn_aggr(mv[:, i], stats[:, i]))
                                        v.tensor_scalar(rstd[:, i:i + 1], mv[:, i, 1:2], EPS, None, ALU.add
                                                        ).then_inc(S["sq"], 1)
                                        v.wait_ge(S["sq"], roots_off + 2 * t + 2)
                                        stand_alone(v, s_up)
                                        ch.link(v.reciprocal(rstd[:, i:i + 1], rstd[:, i:i + 1]))
                                        v.tensor_scalar(out_t, tmp[:], mv[:, i, 0:1], rstd[:, i:i + 1],
                                                        ALU.subtract, ALU.mult).then_inc(S["h"], 1)
                                    else:
                                        v.tensor_scalar(out_t, tmp[:], 0.0, None, ALU.max).then_inc(S["h"], 1)
                                    assert ch.n == links
                                if i >= 2:
                                    t, j = t - 2, i - 2
                                    V = bV[j % 2][:, D:2 * D]
                                    v.wait_ge(S["cp"], n - 1)
                                    v.wait_ge(S["rm"], n - 1)
                                    if kind == "last":
                                        rch.start(2 * t)
                                        v.tensor_tensor(flat(Yh, t).bitcast(F32R), V, bias_r[:], ALU.add
                                                        ).then_inc(S["v2"], 1)
                                        wait(v, S["tr"], n - 1)
                                        v.tensor_tensor(hst[:, j], V, bias_r[:], ALU.add).then_inc(S["v2"], 1)
                                        v.wait_ge(S["v2"], 2 * t + 2)
                                        v.tensor_tensor(flat(Yl, t).bitcast(F32R), hst[:, j], flat(Yh, t),
                                                        ALU.subtract).then_inc(S["vt"], 1)
                                        v.wait_ge(S["vt"], n - 1)
                                        v.tensor_copy(stats[:, j, 0:1], mv[:, j, 0:1]).then_inc(S["r"], 1)
                                    else:
                                        v.tensor_tensor(flat(Yl, t).bitcast(F32R), hst[:, j], flat(Yh, t),
                                                        ALU.subtract).then_inc(S["vt"], 1)
                                        v.tensor_tensor(flat(R, t), V, bias_r[:], ALU.add).then_inc(S["r"], 1)
                        body(1)
                        with v.Fori(2, B) as b:
                            body(b)
                        body(B)

            aggregate(0, "gcn", 0, 1, wview(gW), wview(Wr[0]), bl[0])
            aggregate(1, "sage", 1, 0, wview(Wl[0]), wview(Wr[1]), bl[1])
            aggregate(2, "sage", 0, 1, wview(Wl[1]), wview(Wr[2]), bl[2])
            aggregate(3, "last", 1, 0, wview(Wl[2]), wview(W3), b3)

        with ExitStack() as fc:
            tmp = sb("tmp2", [P, 2, D], c=fc)
            f = {n: sem("f_" + n, fc) for n in "tr ev mm vc sq h rd".split()}
            f_A = [sem(f"f_A{i}", fc) for i in range(2)]
            f_o = [sem(f"f_o{i}", fc) for i in range(2)]
            rows = ring[:].rearrange("p s a c -> p (s a c)")[:, 0:2 * NP].rearrange("p (s c) -> p s c", s=2)
            half = lambda X: X[:].rearrange("p a c -> p (a c)")[:, 0:T * P].rearrange("p (s n) -> p s n", s=T)
            AT_exact = [half(high[1]), half(low[1])]
            R_all = R[:].rearrange("p a c -> p (a c)").rearrange("p (z s n) -> p z s n", z=2, s=T)
            AT_full = [R_all[:, 0], R_all[:, 1]]
            QN = (T + 3) // 4
            rows_v = counts_v.rearrange("b p a c -> p a b c")
            bU = psum[4:6]
            block = fc.enter_context(nc.Block())

            def pairs(eng, body):
                body(0, 0)
                body(1, 1)
                with eng.Fori(1, T // 2) as h:
                    body(2 * h, 0)
                    body(2 * h + 1, 1)
                body(T - 1, 0)

            @block.sync
            def _(sp):
                def load(n, z):
                    wait(sp, f["tr"], QN * (n - 1))
                    sp.dma_start(rows[:, z].rearrange("p (b c) -> p b c", b=HB),
                                 rows_v[:, bass.ds(n, 1), :, :].rearrange("p a b c -> p (a b) c")
                                 ).then_inc(f_A[z], 16)

                pairs(sp, load)

            @block.gpsimd
            def _(pool):
                def store(n, z):
                    pool.wait_ge(f["h"], n + 1)
                    pool.dma_start(out_v[:, bass.ds(n, 1), :].rearrange("p a c -> p (a c)"),
                                   hst[0:NODES // T, z]).then_inc(f_o[z], 16)
                pairs(pool, store)
                pool.wait_ge(f_o[0], 16 * (T // 2 + 1))
                pool.wait_ge(f_o[1], 16 * (T // 2))

            @block.tensor
            def _(pe):
                def products(n, z, q, AT, dt):
                    if q == 0:
                        pe.wait_ge(f["ev"], QN * (n + 1))
                        wait(pe, f["rd"], n - 1)
                    for s in range(4 * q, min(4 * q + 4, T)):
                        for part in (high[0], low[0]):
                            mm = pe.matmul(bU[z][:, 0:D], AT[z][:, s].bitcast(dt), part[:, s].bitcast(dt),
                                           start=(s == 0 and part is high[0]), stop=(s == T - 1 and part is low[0]))
                    if q == QN - 1:
                        mm.then_inc(f["mm"], 1)

                def turn(n, z, q):
                    if q == 0:
                        if isinstance(n, int):
                            pe.wait_ge(f_A[z], 16 * (n // 2 + 1))
                    wait(pe, f["ev"], QN * n + (q - 2 if q < 3 else q - 3))
                    for s in range(4 * q, min(4 * q + 4, T)):
                        mm = pe.transpose(psum[q % 4][:, (s - 4 * q) * P:(s - 4 * q + 1) * P],
                                          rows[:, z, s * P:(s + 1) * P], ident[:])
                    mm.then_inc(f["tr"], 1)

                def tiles(AT, dt):
                    def body(n, z, before=True):
                        for q in range(QN):
                            turn(n, z, q)
                            if before:
                                products(n - 1, 1 - z, q, AT, dt)
                    body(0, 0, False)
                    body(1, 1)
                    with pe.Fori(1, T // 2) as h:
                        pe.wait_ge(f_A[0], 16 * (h + 1))
                        body(2 * h, 0)
                        pe.wait_ge(f_A[1], 16 * (h + 1))
                        body(2 * h + 1, 1)
                    body(T - 1, 0)
                    for q in range(QN):
                        products(T - 1, 0, q, AT, dt)

                exact = pe.value_load(many[0:1, 0:1], min_val=0, max_val=1)
                with pe.If(exact < 1):
                    tiles(AT_exact, F32R)
                with pe.Else():
                    tiles(AT_full, F32)

            @block.scalar
            def _(act):
                def tiles(AT, dt):
                    def root(n, z):
                        act.wait_ge(f["sq"], 2 * n + 1)
                        act.activation(rstd[:, z:z + 1], rstd[:, z:z + 1], ACT.Sqrt).then_inc(f["sq"], 1)

                    def body(n, z):
                        for q in range(QN):
                            w = min(4, T - 4 * q)
                            act.wait_ge(f["tr"], QN * n + q + 1)
                            if q == 0:
                                wait(act, f["mm"], n - 1)
                            act.copy(AT[z][:, 4 * q:4 * q + w].bitcast(dt),
                                     psum[q % 4][:, 0:w * P].rearrange("p (s n) -> p s n", s=w)).then_inc(f["ev"], 1)
                        if not isinstance(n, int) or n >= 2:
                            root(n - 2, z)
                    pairs(act, body)
                    root(T - 2, 1)
                    root(T - 1, 0)

                exact = act.value_load(many[0:1, 0:1], min_val=0, max_val=1)
                with act.If(exact < 1):
                    tiles(AT_exact, F32R)
                with act.Else():
                    tiles(AT_full, F32)

            @block.vector
            def _(v):
                ch = Chain(v, f["vc"])

                def body(n, z):
                    ch.start(n * 3)
                    v.wait_ge(f["mm"], n + 1)
                    wait(v, f["h"], n - 1)
                    v.scalar_tensor_tensor(tmp[:, z], bU[z][:, 0:D], inv_src[:, bass.ds(n, 1)], flat(own, n),
                                           ALU.mult, ALU.add).then_inc(f["rd"], 1)
                    v.wait_ge(f["rd"], n + 1)
                    ch.link(v.bn_stats(stats[:, z], tmp[:, z]))
                    stand_alone(v, s_up)
                    ch.link(v.bn_aggr(mv[:, z], stats[:, z]))
                    v.tensor_scalar(rstd[:, z:z + 1], mv[:, z, 1:2], EPS, None, ALU.add).then_inc(f["sq"], 1)
                    v.wait_ge(f["sq"], 2 * n + 2)
                    stand_alone(v, s_up)
                    ch.link(v.reciprocal(rstd[:, z:z + 1], rstd[:, z:z + 1]))
                    if not isinstance(n, int) or n >= 2:
                        v.wait_ge(f_o[z], 16 * (n // 2) if isinstance(n, int) else 16 * steps[0])
                    v.tensor_scalar(hst[:, z], tmp[:, z], mv[:, z, 0:1], rstd[:, z:z + 1],
                                    ALU.subtract, ALU.mult).then_inc(f["h"], 1)
                steps = [None]
                body(0, 0)
                body(1, 1)
                with v.Fori(1, T // 2) as h:
                    steps[0] = h
                    body(2 * h, 0)
                    body(2 * h + 1, 1)
                body(T - 1, 0)


def kernel(x, src, dst, edge_attr_128, **w):
    import numpy as np
    import concourse.bacc as bacc
    from concourse.bass_utils import run_bass_kernel_spmd

    def padded(a, shape):
        o = np.zeros(shape, a.dtype)
        o[tuple(slice(0, s) for s in a.shape)] = a
        return o

    def edges(a):
        o = np.full(EP, NP - 1, np.int32)
        o[:a.shape[0]] = np.asarray(a)
        return np.ascontiguousarray(o.reshape(G * GC, C).T)

    w = {k: np.asarray(v) for k, v in w.items()}
    xp = padded(np.asarray(x), (NP, D))
    W0 = padded(w["L0_gnn_W0"], (2 * D, H1))
    W1 = padded(w["L0_gnn_W1"], (H1, H2))
    W2b = np.concatenate([w["L0_gnn_W2"], w["L0_gnn_b2"][None]])
    arrays = {
        "xT": np.ascontiguousarray(xp.T),
        "x": xp,
        "src_col": edges(src),
        "dst_col": edges(dst),
        "edge_T": padded(np.asarray(edge_attr_128).T, (P, EP)),
        "W0": W0, "b0": padded(w["L0_gnn_b0"][None], (1, H1)),
        "W1": W1, "b1": np.ascontiguousarray(padded(w["L0_gnn_b1"], (H2,)).reshape(H2T, H2P).T),
        "W2b": W2b, "Wg": w["L0_gnn_Wg"],
        "gW": np.concatenate([w["L1_gnn_W1"], w["L1_gnn_W2"]], axis=1),
        "gb1": w["L1_gnn_b1"][None], "gb2": w["L1_gnn_b2"][None],
    }
    for i in (1, 2, 3):
        arrays[f"Wl{i}"] = np.ascontiguousarray(w[f"L2_gnn_W{i}l"].T)
        arrays[f"Wr{i}"] = np.ascontiguousarray(w[f"L2_gnn_W{i}r"].T)
        arrays[f"bl{i}"] = w[f"L2_gnn_b{i}l"][None]
    arrays["W3"], arrays["b3"] = w["L3_gnn_W"], w["L3_gnn_b"][None]
    nc = bacc.Bacc("TRN2", target_bir_lowering=False, num_devices=1)
    a = {n: nc.dram_tensor("in_" + n, v.shape, mybir.dt.from_np(v.dtype), kind="ExternalInput").ap()
         for n, v in arrays.items()}
    out = nc.dram_tensor("out", (NODES, D), F32, kind="ExternalOutput").ap()
    build(nc, a["xT"], a["x"], a["src_col"], a["dst_col"], a["edge_T"], a["W0"], a["b0"], a["W1"], a["b1"],
          a["W2b"], a["Wg"], a["gW"], a["gb1"], a["gb2"], [a["Wl1"], a["Wl2"], a["Wl3"]],
          [a["bl1"], a["bl2"], a["bl3"]], [a["Wr1"], a["Wr2"], a["Wr3"]], a["W3"], a["b3"], out)
    r = run_bass_kernel_spmd(nc, [{"in_" + n: v for n, v in arrays.items()}], core_ids=[0])
    return r.results[0]["out"]
```

```python
from contextlib import ExitStack

import concourse.bass as bass
from concourse import mybir

F32 = mybir.dt.float32
F32R = mybir.dt.float32r
BF16 = mybir.dt.bfloat16
I32 = mybir.dt.int32
ALU = mybir.AluOpType
ACT = mybir.ActivationFunctionType

P = 128
NODES = 3125
T = 25
NP = P * T
D = 256
KD = D // P
C = 128
GC = 4
G = 104
EP = G * GC * C
H1 = 416
H1F = H1 // P
H1R = H1 - H1F * P
H1T, H1Q = H1F + 1, 3 * H1R
LOW = slice(2 * H1R, H1Q)
H2, H2T, H2P = 324, 3, 108
SW = D + 1
MW = D + 2
B = 5
TB = T // B
BW = TB * P
NW = BW // 2
HB = 2 * B
EXACT = 2048
OB = 16
ON = G * GC // OB
CELLS = NP * NP
EPS = 1e-5
ZERO_AT = (0, 2, 4)
ZW = 13 * SW


def wait(eng, sem, value):
    if not (isinstance(value, int) and value <= 0):
        eng.wait_ge(sem, value)


class Chain:

    def __init__(self, eng, sem):
        self.eng, self.sem, self.base, self.n = eng, sem, 0, 0

    def start(self, base):
        self.base, self.n = base, 0

    def link(self, ins):
        self.note(ins)
        self.settle()

    def note(self, ins):
        self.n += 1
        ins.then_inc(self.sem, 1)

    def settle(self):
        wait(self.eng, self.sem, self.base + self.n)


def stand_alone(eng, s_up):
    eng.sem_inc(s_up)


def looped(eng, n, body, head=1, tail=1):
    for i in range(head):
        body(i)
    with eng.Fori(head, n - tail) as i:
        body(i)
    for i in range(n - tail, n):
        body(i)


def build(nc, xT, x, src_col, dst_col, edge_T, W0, b0, W1, b1, W2b, Wg, gW, gb1, gb2, Wl, bl, Wr, W3, b3, out):
    ctx = ExitStack()
    with ctx:
        def sb(name, shape, dt=F32, c=ctx):
            return c.enter_context(nc.sbuf_tensor(name, shape, dt))

        def sem(name, c=ctx):
            return c.enter_context(nc.semaphore(name))

        def dram(name, shape):
            return nc.dram_tensor(name, shape, F32)

        p_tab, q_tab = dram("p_tab", [NP, H1]), dram("q_tab", [NP, H1])
        sums = dram("sums", [NP + P, SW])
        counts = dram("counts", [CELLS + P, 1])
        sums_v = sums[0:NP, :].rearrange("(p a) w -> p a w", p=P)
        counts_v = counts[0:CELLS, :].rearrange("(b p a c) o -> b p a (c o)", b=HB, p=P, a=T)
        x_v = x.rearrange("(p a) c -> p a c", p=P)
        out_v = out.rearrange("(p a) c -> p a c", a=T)

        psum = [ctx.enter_context(nc.psum_tensor(f"bank{i}", [P, 512], F32)) for i in range(8)]

        s_up = sem("s_up")
        ident = sb("ident", [P, P])
        degree = sb("degree", [P, T])
        inv_src = sb("inv_src", [P, T])
        inv_dst = sb("inv_dst", [P, T])
        dinv = sb("dinv", [P, T])

        with ExitStack() as ec:
            def esb(name, shape, dt=F32):
                return sb(name, shape, dt, ec)

            def esem(name):
                return sem(name, ec)

            lower = esb("lower", [P, P])
            src_i = esb("src_i", [P, G * GC], I32)
            dst_i = esb("dst_i", [P, G * GC], I32)
            cells = esb("cells", [P, G * GC, 2])
            digits = esb("digits", [P, G * GC, 2])
            iota_p = esb("iota_p", [P, P])
            trash = esb("trash", [P, 2])
            w1, w1h, w1l = (esb(n, [P, H1T, H2]) for n in ("w1", "w1h", "w1l"))
            w2, w2h, w2l = (esb(n, [H2P, H2T, D]) for n in ("w2", "w2h", "w2l"))
            zeros = esb("zeros", [P, ZW])
            s_zd = esem("s_zd")
            n_zero = CELLS // (P * NP)
            flat_counts = counts[0:CELLS, :].rearrange("(m p c) o -> m p (c o)", p=P, c=NP)

            def clear_counts(eng, m):
                eng.dma_start(flat_counts[bass.ds(m, 1), :, :].rearrange("m p c -> (m p) c"), zeros[:, 0:NP]
                              ).then_inc(s_zd, 16)
            wg = esb("wg", [P, D])
            b1c = esb("b1c", [H2P, H2T])
            hidden1, hidden1h, hidden1l = (esb(n, [P, H1T, GC * C]) for n in ("hidden1", "hidden1h", "hidden1l"))
            hidden2, hidden2h, hidden2l = (esb(n, [H2P, H2T, GC * C]) for n in ("hidden2", "hidden2h", "hidden2l"))

            with ExitStack() as sc:
                def ssb(name, shape, dt=F32):
                    return sb(name, shape, dt, sc)

                def ssem(name):
                    return sem(name, sc)

                oh_p = ssb("oh_p", [P, TB, OB, P], BF16)
                oh_t = ssb("oh_t", [P, TB, OB, T], BF16)
                bf = ssb("bf", [P, G * GC])
                w0 = ssb("w0", [P, 2 * KD, H1])
                b0_b = ssb("b0_b", [P, H1])
                xt = ssb("xt", [P, TB, KD, P])
                p_out = ssb("p_out", [P, TB, H1])
                q_out = ssb("q_out", [P, TB, H1])
                sf = ssb("sf", [P, G * GC])
                df = ssb("df", [P, G * GC])
                qi = ssb("qi", [P, G * GC], I32)
                qf = ssb("qf", [P, G * GC])
                rf = ssb("rf", [P, G * GC])
                mf = ssb("mf", [P, G * GC])
                s_zero, s_w, s_idx = ssem("s_zero"), ssem("s_w"), ssem("s_idx")
                s_oh, s_deg, s_hi = ssem("s_oh"), ssem("s_deg"), ssem("s_hi")
                s_cg, s_cd = ssem("s_cg"), ssem("s_cd")
                s_pq, s_pe, s_qe = ssem("s_pq"), ssem("s_pe"), ssem("s_qe")
                s_xt = [ssem(f"s_xt{j}") for j in range(TB)]
                s_po = [ssem(f"s_po{j}") for j in range(TB)]
                s_qo = [ssem(f"s_qo{j}") for j in range(TB)]
                s_wl = ssem("s_wl")
                xT_v = xT.rearrange("(k p) n -> p k n", p=P)
                block = sc.enter_context(nc.Block())

                @block.sync
                def _(sp):
                    sp.dma_start(src_i[:], src_col).then_inc(s_idx, 16)
                    sp.dma_start(dst_i[:], dst_col).then_inc(s_idx, 16)
                    sp.dma_start(w0[:], W0.rearrange("(k p) n -> p k n", p=P)).then_inc(s_w, 16)
                    sp.dma_start(b0_b[:], b0.broadcast_to([P, H1])).then_inc(s_w, 16)

                    def load(n, j):
                        sp.dma_start(xt[:, j], xT_v[:, :, bass.ds(n * P, P)]).then_inc(s_xt[j], 16)

                    def body(b):
                        for j in range(TB):
                            n = b * TB + j
                            sp.wait_ge(s_pe, n + 1)
                            sp.dma_start(p_tab[bass.ds(n * P, P), :], p_out[:, j]).then_inc(s_po[j], 16)
                            sp.wait_ge(s_qe, n + 1)
                            sp.dma_start(q_tab[bass.ds(n * P, P), :], q_out[:, j]).then_inc(s_qo[j], 16)
                            if not (isinstance(b, int) and b == B - 1):
                                sp.wait_ge(s_pq, n + 1)
                                load(n + TB, j)
                    for j in range(TB):
                        load(j, j)
                    looped(sp, B, body)
                    for j in range(TB):
                        sp.wait_ge(s_po[j], 16 * B)
                        sp.wait_ge(s_qo[j], 16 * B)

                @block.tensor
                def _(pe):
                    pe.wait_ge(s_w, 32)

                    def degrees(n, slot):
                        pe.wait_ge(s_oh, n + 1)
                        for c in range(OB):
                            mm = pe.matmul(psum[6][:, 0:T], oh_p[:, slot, c], oh_t[:, slot, c],
                                           start=(isinstance(n, int) and n == 0 and c == 0),
                                           stop=(isinstance(n, int) and n == ON - 1 and c == OB - 1),
                                           skip_group_check=True)
                        mm.then_inc(s_deg, 1)

                    def body(b):
                        for j in range(TB):
                            n = b * TB + j
                            pe.wait_ge(s_xt[j], 16 * (b + 1))
                            before = {0: n - 2, 1: n - 2, 2: n - 5, 3: n - 3, 4: n - 3}[j]
                            wait(pe, s_pe, before + 1)
                            wait(pe, s_qe, before + 1)
                            for half in range(2):
                                for k in range(KD):
                                    mm = pe.matmul(psum[2 * (j % 3) + half][:, 0:H1], xt[:, j, k], w0[:, 2 * half + k],
                                                   start=(k == 0), stop=(k == KD - 1))
                            mm.then_inc(s_pq, 1)
                            degrees(n, j)
                    looped(pe, B, body)
                    degrees(T, 0)

                @block.scalar
                def _(act):
                    act.dma_start(w1[:, 0:H1F], W1[0:H1F * P, :].rearrange("(k p) n -> p k n", p=P)).then_inc(s_wl, 16)
                    for i in range(3):
                        act.dma_start(w1[i * H1R:(i + 1) * H1R, H1F], W1[H1F * P:H1, :]).then_inc(s_wl, 16)
                    act.dma_start(w2[:], W2b.rearrange("(k p) n -> p k n", p=H2P)).then_inc(s_wl, 16)
                    act.dma_start(wg[:], Wg).then_inc(s_wl, 16)
                    act.dma_start(b1c[:], b1).then_inc(s_wl, 16)
                    act.wait_ge(s_zero, 1)
                    for m in range(3):
                        clear_counts(act, m)

                    def body(b):
                        for j in range(TB):
                            n = b * TB + j
                            act.wait_ge(s_pq, n + 1)
                            wait(act, s_po[j], 16 * b)
                            act.copy(p_out[:, j], psum[2 * (j % 3)][:, 0:H1]).then_inc(s_pe, 1)
                            if j in ZERO_AT:
                                clear_counts(act, 3 + b * len(ZERO_AT) + ZERO_AT.index(j))
                    looped(act, B, body)
                    for m in range(3):
                        clear_counts(act, 3 + B * len(ZERO_AT) + m)
                    act.wait_ge(s_wl, 7 * 16)
                    act.copy(w1h[:, 0:H1F].bitcast(F32R), w1[:, 0:H1F]).then_inc(s_hi, 1)
                    act.copy(w1h[0:H1Q, H1F].bitcast(F32R), w1[0:H1Q, H1F]).then_inc(s_hi, 1)
                    act.copy(w2h[:].bitcast(F32R), w2[:]).then_inc(s_hi, 1)

                @block.gpsimd
                def _(pool):
                    pool.memset(ident[:], 0.0).then_inc(s_cg, 1)
                    pool.memset(lower[:], 1.0).then_inc(s_cg, 1)
                    pool.wait_ge(s_cg, 2)
                    pool.affine_select(out=ident[:], in_=ident[:], compare_op=ALU.not_equal, fill=1.0, base=0,
                                       pattern=[[-1, P]], channel_multiplier=1).then_inc(s_cg, 1)
                    pool.affine_select(out=lower[:], in_=lower[:], compare_op=ALU.is_gt, fill=0.0, base=0,
                                       pattern=[[-1, P]], channel_multiplier=1).then_inc(s_cg, 1)
                    pool.iota(iota_p[:], [[1, P]], base=0, channel_multiplier=0,
                              allow_small_or_imprecise_dtypes=True).then_inc(s_cg, 1)
                    pool.iota(trash[:, 0:1], [[0, 1]], base=NP, channel_multiplier=1,
                              allow_small_or_imprecise_dtypes=True).then_inc(s_cg, 1)
                    pool.iota(trash[:, 1:2], [[0, 1]], base=CELLS, channel_multiplier=1,
                              allow_small_or_imprecise_dtypes=True).then_inc(s_cg, 1)
                    pool.wait_ge(s_cg, 7)

                @block.vector
                def _(v):
                    v.memset(zeros[:], 0.0).then_inc(s_zero, 1)
                    ch = Chain(v, s_cd)
                    v.wait_ge(s_idx, 32)
                    ch.link(v.tensor_copy(df[:], dst_i[:]))
                    ch.link(v.tensor_copy(sf[:], src_i[:]))
                    ch.link(v.tensor_scalar(qi[:], df[:], 1.0 / T, -0.48, ALU.mult, ALU.add))
                    ch.link(v.tensor_copy(qf[:], qi[:]))
                    ch.link(v.scalar_tensor_tensor(rf[:], qf[:], -float(T), df[:], ALU.mult, ALU.add))
                    ch.link(v.tensor_scalar(mf[:], rf[:], float(T), None, ALU.is_ge))
                    ch.link(v.tensor_tensor(qf[:], qf[:], mf[:], ALU.add))
                    ch.link(v.scalar_tensor_tensor(rf[:], mf[:], -float(T), rf[:], ALU.mult, ALU.add))
                    ch.link(v.tensor_scalar(mf[:], rf[:], 0.0, None, ALU.is_lt))
                    ch.link(v.tensor_tensor(qf[:], qf[:], mf[:], ALU.subtract))
                    ch.link(v.scalar_tensor_tensor(rf[:], mf[:], float(T), rf[:], ALU.mult, ALU.add))
                    ch.link(v.tensor_copy(digits[:, :, 0], qf[:]))
                    ch.link(v.tensor_copy(digits[:, :, 1], rf[:]))
                    ch.link(v.scalar_tensor_tensor(qf[:], rf[:], float(P), qf[:], ALU.mult, ALU.add))
                    ch.link(v.tensor_scalar(bf[:], qf[:], float(NW), None, ALU.is_ge))
                    for k in range(2, HB):
                        ch.link(v.scalar_tensor_tensor(bf[:], qf[:], float(NW * k), bf[:], ALU.is_ge, ALU.add))
                    ch.link(v.scalar_tensor_tensor(qf[:], bf[:], float((NP - 1) * NW), qf[:], ALU.mult, ALU.add))
                    ch.link(v.scalar_tensor_tensor(qf[:], sf[:], float(NW), qf[:], ALU.mult, ALU.add))
                    ch.link(v.tensor_copy(cells[:, :, 0], sf[:]))
                    ch.link(v.tensor_copy(cells[:, :, 1], qf[:]))
                    v.wait_ge(s_w, 32)

                    v.wait_ge(s_cg, 7)

                    def one_hots(n, slot):
                        wait(v, s_deg, n - TB + 1)
                        at = bass.ds(n * OB, OB)
                        v.tensor_tensor(oh_p[:, slot], iota_p[:].unsqueeze(1).broadcast_to([P, OB, P]),
                                        digits[:, at, 0:1].broadcast_to([P, OB, P]), ALU.is_equal)
                        v.tensor_tensor(oh_t[:, slot], iota_p[:, 0:T].unsqueeze(1).broadcast_to([P, OB, T]),
                                        digits[:, at, 1:2].broadcast_to([P, OB, T]), ALU.is_equal).then_inc(s_oh, 1)

                    def body(b):
                        for j in range(TB):
                            n = b * TB + j
                            one_hots(n, j)
                            v.wait_ge(s_pq, n + 1)
                            wait(v, s_qo[j], 16 * b)
                            v.tensor_tensor(q_out[:, j], psum[2 * (j % 3) + 1][:, 0:H1], b0_b[:],
                                            ALU.add).then_inc(s_qe, 1)
                    looped(v, B, body)
                    one_hots(T, 0)
                    v.wait_ge(s_hi, 3)
                    v.tensor_tensor(w1l[:, 0:H1F].bitcast(F32R), w1[:, 0:H1F], w1h[:, 0:H1F], ALU.subtract)
                    mid = slice(H1R, 2 * H1R)
                    v.tensor_tensor(w1h[mid, H1F].bitcast(F32R), w1[mid, H1F], w1h[mid, H1F], ALU.subtract)
                    v.tensor_tensor(w2l[:].bitcast(F32R), w2[:], w2h[:], ALU.subtract)
                    v.wait_ge(s_deg, ON)
                    v.tensor_copy(degree[:], psum[6][:, 0:T])

            p_in = esb("p_in", [P, GC, H1])
            q_in = esb("q_in", [P, GC, H1])
            pre1 = esb("pre1", [P, GC, H1T * P])
            gidx = esb("gidx", [P, 2, GC], I32)
            keys = esb("keys", [P, GC, 2])
            eT = esb("eT", [P, GC * C])
            same = esb("same", [P, GC, C])
            junk, junk2, junk3 = (esb(n, [P, GC, C]) for n in ("junk", "junk2", "junk3"))
            before = esb("before", [P, GC, 2])
            number = esb("number", [P, GC])
            later = esb("later", [P, GC, 2])
            away = esb("away", [P, GC, 2])
            gated = esb("gated", [P, GC, 2 * D])
            msg = esb("msg", [P, GC, D])
            msgh, msgl = esb("msgh", [P, GC, MW]), esb("msgl", [P, GC, MW])
            msum = esb("msum", [P, GC, SW])
            number_out = esb("number_out", [P, GC])
            sidx = esb("sidx", [P, GC, 2], I32)

            s_gp = [esem(f"s_gp{c}") for c in range(GC)]
            s_gq = [esem(f"s_gq{c}") for c in range(GC)]
            s_idxp = esem("s_idxp")
            s_idxq = esem("s_idxq")
            s_add = esem("s_add")
            s_T = esem("s_T")
            s_th1 = esem("s_th1")
            s_L1 = esem("s_L1")
            s_th2 = esem("s_th2")
            s_L2 = esem("s_L2")
            s_gt = esem("s_gt")
            s_msg = esem("s_msg")
            s_S = esem("s_S")
            s_sev = esem("s_sev")
            s_MR = esem("s_MR")
            s_M = esem("s_M")
            s_lo1 = esem("s_lo1")
            s_lo2 = esem("s_lo2")
            s_lom = esem("s_lom")
            s_him = esem("s_him")
            s_ks = esem("s_ks")
            s_fin = esem("s_fin")
            s_sums = esem("s_sums")
            s_cnt = esem("s_cnt")
            s_eT = esem("s_eT")
            s_vc = esem("s_vc")
            s_one = esem("s_one")
            bT, bH, bO, bM = psum[0:2], psum[2:4], psum[4:6], psum[6:8]
            bS = bO + bM
            blk = ec.enter_context(nc.Block())

            def edge_loop(eng, body, after_first=None, unroll=1):
                body(0, True, False)
                if after_first:
                    after_first()
                body(1, True, True)
                assert (G - 2) % unroll == 0
                with eng.Fori(0, (G - 2) // unroll) as i:
                    for u in range(unroll):
                        body(unroll * i + (2 + u), True, True)
                body(G, False, True)

            @blk.sync
            def _(sp):
                def body(g, front, back):
                    if front:
                        wait(sp, s_L2, g * GC)
                        sp.dma_start(eT[:], edge_T[:, bass.ds(g * (GC * C), GC * C)]).then_inc(s_eT, 16)
                def zeros_left():
                    sp.wait_ge(s_gq[GC - 1], 16)
                    left = list(range(B * len(ZERO_AT) + 6, n_zero))
                    for m in left[:2]:
                        clear_counts(sp, m)
                    sp.dma_start(counts[CELLS:CELLS + P, :], zeros[:, 0:1]).then_inc(s_zd, 16)
                    for m in range(2):
                        sp.dma_start(sums[m * 1664:(m + 1) * 1664, :].rearrange("(p a) w -> p (a w)", p=P),
                                     zeros[:]).then_inc(s_zd, 16)
                    sp.wait_ge(s_gq[GC - 1], 32)
                    for m in left[2:]:
                        clear_counts(sp, m)

                edge_loop(sp, body, zeros_left)

            @blk.gpsimd
            def _(pool):
                def gather(c, tab, rows_in, which, done):
                    pool.indirect_dma_start(out=rows_in[:, c], out_offset=None, in_=tab[:],
                                            in_offset=bass.IndirectOffsetOnAxis(ap=gidx[:, which, c:c + 1], axis=0)
                                            ).then_inc(done[c], 16)

                def scatter(g, c):
                    n = g * GC + c
                    if c == 0:
                        pool.wait_ge(s_fin, g + 1)
                    wait(pool, s_cnt, 16 * n)
                    stand_alone(pool, s_up)
                    pool.indirect_dma_start(out=counts[:], in_=number_out[:, c:c + 1], in_offset=None,
                                            out_offset=bass.IndirectOffsetOnAxis(ap=sidx[:, c, 1:2], axis=0),
                                            compute_op=ALU.add).then_inc(s_cnt, 16)
                    pool.wait_ge(s_sev, n + 1)
                    wait(pool, s_sums, 16 * n)
                    stand_alone(pool, s_up)
                    pool.indirect_dma_start(out=sums[:], in_=msum[:, c], in_offset=None,
                                            out_offset=bass.IndirectOffsetOnAxis(ap=sidx[:, c, 0:1], axis=0),
                                            compute_op=ALU.add).then_inc(s_sums, 16)

                def body(g_in, g_out):
                    for c in range(GC):
                        if g_in is not None:
                            if c == 0:
                                pool.wait_ge(s_idxp, g_in + 1)
                            wait(pool, s_add, (g_in - 1) * GC + c + 1)
                            stand_alone(pool, s_up)
                            gather(c, p_tab, p_in, 0, s_gp)
                    for c in range(GC):
                        if g_out is not None:
                            scatter(g_out, c)
                        if g_in is not None:
                            if c == 0:
                                pool.wait_ge(s_idxq, g_in + 1)
                                stand_alone(pool, s_up)
                            gather(c, q_tab, q_in, 1, s_gq)
                body(0, None)
                body(1, None)
                body(2, None)
                pool.wait_ge(s_zd, 16 * (n_zero + 3))
                with pool.Fori(2, G - 1) as g:
                    body(g + 1, g - 2)
                for g in range(G - 3, G):
                    body(None, g)
                pool.wait_ge(s_sums, 16 * G * GC)
                pool.wait_ge(s_cnt, 16 * G * GC)

            @blk.tensor
            def _(pe):
                def transposes(g, c):
                    n = g * GC + c
                    pe.wait_ge(s_add, n + 1)
                    wait(pe, s_th1, n - 1)
                    for k in range(H1T):
                        mm = pe.transpose(bT[c % 2][:, k * C:(k + 1) * C], pre1[:, c, k * P:(k + 1) * P], ident[:])
                    mm.then_inc(s_T, 1)

                def split_product(out, lhs, rhs, first, last):
                    (lh, ll), (rh, rl) = lhs, rhs
                    pe.matmul(out, lh.bitcast(F32R), rh.bitcast(F32R), start=first, stop=False)
                    pe.matmul(out, lh.bitcast(F32R), rl.bitcast(F32R), start=False, stop=False)
                    return pe.matmul(out, ll.bitcast(F32R), rh.bitcast(F32R), start=False, stop=last)

                def first(g, m):
                    wait(pe, s_th2, H2T * g + m - 1 if m == 2 else H2T * g)
                    cols = slice(m * H2P, (m + 1) * H2P)
                    for k in range(H1F):
                        split_product(bH[m % 2][0:H2P, :], (w1h[:, k, cols], w1l[:, k, cols]),
                                      (hidden1h[:, k], hidden1l[:, k]), k == 0, False)
                    pe.matmul(bH[m % 2][0:H2P, :], w1h[0:H1Q, H1F, cols].bitcast(F32R),
                              hidden1h[0:H1Q, H1F].bitcast(F32R), start=False, stop=True).then_inc(s_L1, 1)

                def second(g, c):
                    if c >= 2:
                        pe.wait_ge(s_gt, (g - 1) * GC + c - 1)
                    e = slice(c * C, (c + 1) * C)
                    for k in range(H2T):
                        split_product(bO[c % 2][:, 0:D], (hidden2h[:, k, e], hidden2l[:, k, e]),
                                      (w2h[:, k], w2l[:, k]), k == 0, k == H2T - 1)
                    pe.matmul(bO[c % 2][:, D:2 * D], eT[:, e], wg[:], start=True, stop=True).then_inc(s_L2, 1)

                def body(g, front, back):
                    if front:
                        transposes(g, 0)
                        transposes(g, 1)
                    if back:
                        pe.wait_ge(s_ks, g)
                        wait(pe, s_sev, (g - 1) * GC)
                        for c in range(GC):
                            for s in range(2):
                                at = (c % 2) * 2 * C + s * C
                                mm = pe.transpose(bM[c // 2][:, at:at + C],
                                                  keys[:, c, s:s + 1].broadcast_to([P, P]), ident[:])
                            mm.then_inc(s_MR, 1)
                    if front:
                        transposes(g, 2)
                    if back:
                        pe.wait_ge(s_th2, H2T * g)
                        pe.wait_ge(s_lo2, H2T * g)
                        pe.wait_ge(s_eT, 16 * g)
                        second(g, 0)
                    if front:
                        transposes(g, 3)
                    if back:
                        for c in range(1, GC):
                            second(g, c)
                    if front:
                        pe.wait_ge(s_th1, (g + 1) * GC)
                        pe.wait_ge(s_lo1, (g + 1) * GC)
                        for m in range(H2T - 1):
                            first(g, m)
                    if back:
                        pe.wait_ge(s_M, g * GC)
                        pe.wait_ge(s_him, g * GC)
                        pe.wait_ge(s_lom, g * GC)
                        pe.wait_ge(s_gt, g * GC)
                        for c in range(GC):
                            eq = same[:, c].bitcast(F32R)
                            pe.matmul(bS[c][:, 0:MW], eq, msgh[:, c].bitcast(F32R), start=True, stop=False)
                            pe.matmul(bS[c][:, 0:MW], eq, msgl[:, c].bitcast(F32R), start=False,
                                      stop=True).then_inc(s_S, 1)
                    if front:
                        first(g, H2T - 1)
                edge_loop(pe, body, unroll=2)

            @blk.scalar
            def _(act):
                act.wait_ge(s_one, 4)

                def body(g, front, back):
                    def gated_out(c):
                        n = (g - 1) * GC + c
                        act.wait_ge(s_L2, n + 1)
                        wait(act, s_msg, n - GC + 1)
                        act.copy(gated[:, c], bO[c % 2][:, :]).then_inc(s_gt, 1)

                    if front:
                        wait(act, s_L1, H2T * g)
                        wait(act, s_lo1, GC * g)
                        for c in range(GC):
                            n = g * GC + c
                            if back and c == GC - 1:
                                gated_out(0)
                            e = slice(c * C, (c + 1) * C)
                            act.wait_ge(s_T, n + 1)
                            src = bT[c % 2][:, :].rearrange("p (k e) -> p k e", k=H1T)
                            act.activation(hidden1[:, :, e], src, ACT.Tanh)
                            act.activation(hidden1h[:, :, e].bitcast(F32R), src, ACT.Tanh).then_inc(s_th1, 1)
                    if back:
                        for c in range(1 if front else 0, GC):
                            gated_out(c)
                        wait(act, s_S, GC * (g - 1))
                        wait(act, s_lom, GC * (g - 1))
                        for c in range(GC):
                            act.wait_ge(s_msg, (g - 1) * GC + c + 1)
                            act.copy(msgh[:, c, 0:D].bitcast(F32R), msg[:, c]).then_inc(s_him, 1)
                    def second_tanh(m):
                        rows = H2P - 1 if m == H2T - 1 else H2P
                        act.wait_ge(s_L1, H2T * g + m + 1)
                        act.activation(hidden2[0:rows, m], bH[m % 2][0:rows, :], ACT.Tanh, bias=b1c[0:rows, m:m + 1])
                        act.activation(hidden2h[0:rows, m].bitcast(F32R), bH[m % 2][0:rows, :], ACT.Tanh,
                                       bias=b1c[0:rows, m:m + 1]).then_inc(s_th2, 1)
                    if front:
                        wait(act, s_L2, GC * g)
                        wait(act, s_lo2, H2T * g)
                        for m in range(H2T - 1):
                            second_tanh(m)
                    if back:
                        for c in range(GC):
                            n = (g - 1) * GC + c
                            act.wait_ge(s_S, n + 1)
                            wait(act, s_sums, 16 * (n - GC + 1))
                            act.copy(msum[:, c], bS[c][:, 0:SW]).then_inc(s_sev, 1)
                    if front:
                        second_tanh(H2T - 1)
                edge_loop(act, body)

            @blk.vector
            def _(v):
                ch = Chain(v, s_vc)
                per_group = 4

                def sender_rows(g):
                    v.tensor_copy(gidx[:, 0], src_i[:, bass.ds(g * GC, GC)]).then_inc(s_idxp, 1)

                def receiver_rows(g):
                    v.tensor_copy(gidx[:, 1], dst_i[:, bass.ds(g * GC, GC)]).then_inc(s_idxq, 1)

                def adds(g, chunks, more=True):
                    for c in chunks:
                        if c == 0:
                            for i in range(GC):
                                v.wait_ge(s_gp[i], 16 * (g + 1))
                            if more:
                                sender_rows(g + 1)
                        v.wait_ge(s_gq[c], 16 * (g + 1))
                        wait(v, s_T, (g - 1) * GC + c + 1)
                        if c == GC - 1 and more:
                            receiver_rows(g + 1)
                        full, rest = slice(0, H1F * P), slice(H1F * P, H1)
                        v.tensor_tensor(pre1[:, c, full], p_in[:, c, full], q_in[:, c, full], ALU.add)
                        copies = [P, P // H1R, H1R]
                        v.tensor_tensor(pre1[:, c, H1F * P:].rearrange("p (r n) -> p r n", n=H1R),
                                        p_in[:, c, rest].unsqueeze(1).broadcast_to(copies),
                                        q_in[:, c, rest].unsqueeze(1).broadcast_to(copies), ALU.add
                                        ).then_inc(s_add, 1)

                def compare(g, c):
                    n = (g - 1) * GC + c
                    at = (c % 2) * 2 * C
                    row_s, row_k = bM[c // 2][:, at:at + C], bM[c // 2][:, at + C:at + 2 * C]
                    v.wait_ge(s_MR, (g - 1) * GC + 2 * (c // 2) + 2)
                    wait(v, s_S, n - GC + 1)
                    v.tensor_scalar(same[:, c].bitcast(F32R), row_s, keys[:, c, 0:1], None, ALU.is_equal)
                    v.scalar_tensor_tensor(junk[:, c], row_s, keys[:, c, 0:1], lower[:],
                                           ALU.is_equal, ALU.mult, accum_out=before[:, c, 0:1])
                    v.scalar_tensor_tensor(junk2[:, c], row_k, keys[:, c, 1:2], lower[:],
                                           ALU.is_equal, ALU.mult, accum_out=before[:, c, 1:2])
                    v.tensor_scalar(junk3[:, c], row_k, keys[:, c, 1:2], None, ALU.is_equal,
                                    ALU.add, accum_out=number[:, c:c + 1]).then_inc(s_M, 1)

                def body(g, front, back, more=2):
                    def cells_out():
                        if back:
                            wait(v, s_cnt, 16 * GC * (g - 1))
                            wait(v, s_sums, 16 * GC * (g - 1))
                            ch.link(v.tensor_tensor(sidx[:], away[:], keys[:], ALU.add))
                            v.tensor_copy(number_out[:], number[:]).then_inc(s_fin, 1)
                        if front:
                            v.tensor_copy(keys[:], cells[:, bass.ds(g * GC, GC), :]).then_inc(s_ks, 1)
                    for c in range(GC):
                        if back:
                            compare(g, c)
                        if front:
                            n = g * GC + c
                            e = slice(c * C, (c + 1) * C)
                            v.wait_ge(s_th1, n + 1)
                            if c == 0:
                                wait(v, s_L1, H2T * g)
                            full = slice(0, H1F)
                            v.tensor_tensor(hidden1l[:, full, e].bitcast(F32R), hidden1[:, full, e],
                                            hidden1h[:, full, e], ALU.subtract)
                            v.tensor_tensor(hidden1h[LOW, H1F, e].bitcast(F32R), hidden1[LOW, H1F, e],
                                            hidden1h[LOW, H1F, e], ALU.subtract).then_inc(s_lo1, 1)
                    if back:
                        ch.start((g - 1) * per_group)
                        for c in range(GC):
                            n = (g - 1) * GC + c
                            v.wait_ge(s_gt, n + 1)
                            wait(v, s_him, n - GC + 1)
                            wait(v, s_lom, n - GC + 1)
                            v.tensor_tensor(msg[:, c], gated[:, c, 0:D], gated[:, c, D:2 * D],
                                            ALU.mult).then_inc(s_msg, 1)
                        for c in range(GC):
                            n = (g - 1) * GC + c
                            v.wait_ge(s_him, n + 1)
                            v.tensor_tensor(msgl[:, c, 0:D].bitcast(F32R), msg[:, c], msgh[:, c, 0:D],
                                            ALU.subtract).then_inc(s_lom, 1)
                        v.wait_ge(s_M, g * GC)
                        ch.link(v.tensor_scalar(later[:], before[:], 0.5, None, ALU.is_ge))
                        ch.link(v.scalar_tensor_tensor(away[:], keys[:], -1.0,
                                                       trash[:].unsqueeze(1).broadcast_to([P, GC, 2]),
                                                       ALU.mult, ALU.add))
                        ch.link(v.tensor_tensor(away[:], away[:], later[:], ALU.mult))
                    if front:
                        for m in range(H2T):
                            if more > 0:
                                adds(g + 1, ([0, 1], [2, 3], [])[m], more > 1)
                            if m == 1:
                                cells_out()
                            rows_m = H2P - 1 if m == H2T - 1 else H2P
                            v.wait_ge(s_th2, H2T * g + m + 1)
                            if m == 0:
                                wait(v, s_L2, GC * g)
                            v.tensor_tensor(hidden2l[0:rows_m, m].bitcast(F32R), hidden2[0:rows_m, m],
                                            hidden2h[0:rows_m, m], ALU.subtract).then_inc(s_lo2, 1)
                    else:
                        cells_out()

                v.memset(msgh[:], 1.0).then_inc(s_one, 1)
                v.memset(msgl[:], 0.0).then_inc(s_one, 1)
                v.memset(hidden2h[:], 1.0).then_inc(s_one, 1)
                v.memset(hidden2l[:], 0.0).then_inc(s_one, 1)
                sender_rows(0)
                receiver_rows(0)
                adds(0, range(GC))
                v.wait_ge(s_one, 4)
                body(0, True, False)
                body(1, True, True)
                with v.Fori(2, G - 2) as g:
                    body(g, True, True)
                body(G - 2, True, True, 1)
                body(G - 1, True, True, 0)
                body(G, False, True, 0)

        parts = [sb(f"parts{i}", [P, 2, T, D]) for i in range(2)]
        high, low = [p[:, 0] for p in parts], [p[:, 1] for p in parts]
        own = sb("own", [P, T, D])
        R = sb("R", [P, T, D])
        hst = sb("hst", [P, TB, D])
        hT = sb("hT", [P, 2, KD, P])
        stats = sb("stats", [P, TB, 6])
        mv = sb("mv", [P, TB, 2])
        rstd = sb("rstd", [P, TB])
        w_l = sb("w_l", [P, KD, 2 * D])
        w_r = sb("w_r", [P, KD, D])
        bias_r = sb("bias_r", [P, D])
        many = sb("many", [1, 1], I32)

        def flat(X, t):
            return X[:, bass.ds(t, 1), :].rearrange("p a c -> p (a c)")

        with ExitStack() as lc:
            tab = (parts[1][:].rearrange("p z a c -> p (z a c)")[:, 0:T * SW]
                   .rearrange("p (a w) -> p a w", w=SW))
            xs = sb("xs", [P, TB, D], c=lc)
            tmp = sb("tmp", [P, TB, D], c=lc)
            bias_l = sb("bias_l", [P, 2, D], c=lc)
            most = sb("most", [P, 4], c=lc)
            names1 = "wt v v2 sq h x cp tr xt rm r lo mx mt".split()
            tmp2 = sb("own_part", [P, TB, D], c=lc)
            N1 = {n: sem("n_" + n, lc) for n in names1}
            n_t = [sem(f"n_t{j}", lc) for j in range(2)]
            bU, bMost, bV = psum[0:TB], psum[5], psum[6:8]
            block = lc.enter_context(nc.Block())

            def norm_loop(eng, body):
                body(0)
                with eng.Fori(1, B) as b:
                    body(b)

            @block.sync
            def _(sp):
                for b in range(B):
                    at = slice(b * TB, (b + 1) * TB)
                    sp.dma_start(tab[:, at], sums_v[:, at]).then_inc(n_t[min(b, 1)], 16)
                    sp.dma_start(own[:, at], x_v[:, at]).then_inc(n_t[min(b, 1)], 16)

            @block.scalar
            def _(act):
                act.dma_start(w_l[:], gW.rearrange("(k p) n -> p k n", p=P)).then_inc(N1["wt"], 16)
                for q, row in enumerate((gb1, gb2)):
                    act.dma_start(bias_l[:, q], row.broadcast_to([P, D])).then_inc(N1["wt"], 16)
                act.wait_ge(N1["sq"], 1)
                act.activation(dinv[:], dinv[:], ACT.Sqrt).then_inc(N1["sq"], 1)

                def body(b):
                    act.wait_ge(N1["sq"], 2 * b + 3)
                    act.activation(rstd[:], rstd[:], ACT.Sqrt).then_inc(N1["sq"], 1)
                    for i in range(TB + 1):
                        n = b * TB + i
                        if i < TB:
                            act.wait_ge(N1["h"], n + 1)
                            wait(act, N1["lo"], n - TB + 1)
                            d = dinv[:, bass.ds(n, 1)]
                            act.activation(xs[:, i], hst[:, i], ACT.Copy, scale=d).then_inc(N1["x"], 1)
                            act.activation(flat(high[0], n).bitcast(F32R), hst[:, i], ACT.Copy, scale=d
                                           ).then_inc(N1["cp"], 1)
                        if i >= 1:
                            act.wait_ge(N1["tr"], n)
                            wait(act, N1["rm"], n - 1 if i == 1 else n - 2)
                            act.copy(hT[:, (i - 1) % 2], bV[(i - 1) % 2][:, 0:D].rearrange("p (k n) -> p k n", k=KD)
                                     ).then_inc(N1["xt"], 1)
                norm_loop(act, body)

            @block.tensor
            def _(pe):
                pe.wait_ge(N1["wt"], 48)
                pe.wait_ge(N1["mx"], 1)
                pe.transpose(bMost[0:1, 0:P], most[:, 0:1], ident[:]).then_inc(N1["mt"], 1)

                def tr(n, i):
                    pe.wait_ge(N1["x"], n + 1)
                    wait(pe, N1["xt"], n if i == 0 else n - 1)
                    for k in range(KD):
                        mm = pe.transpose(bV[i % 2][:, k * P:(k + 1) * P], xs[:, i, k * P:(k + 1) * P], ident[:])
                    mm.then_inc(N1["tr"], 1)

                def rm(n, i):
                    pe.wait_ge(N1["xt"], n + 1)
                    wait(pe, N1["r"], n - TB + 1)
                    for k in range(KD):
                        mm = pe.matmul(bU[i][:, :], hT[:, i % 2, k], w_l[:, k], start=(k == 0), stop=(k == KD - 1))
                    mm.then_inc(N1["rm"], 1)

                def body(b):
                    for i in range(TB + 1):
                        if i < TB:
                            tr(b * TB + i, i)
                        if i >= 1:
                            rm(b * TB + i - 1, i - 1)
                norm_loop(pe, body)

            @block.gpsimd
            def _(pool):
                def own_parts(b):
                    for i in range(TB):
                        m = b * TB + i
                        pool.wait_ge(N1["cp"], m + 1)
                        pool.wait_ge(N1["v2"], m + 1)
                        pool.tensor_tensor(flat(own, m), tmp2[:, i], hst[:, i], ALU.add)
                        pool.tensor_tensor(flat(low[0], m).bitcast(F32R), xs[:, i], flat(high[0], m), ALU.subtract
                                           ).then_inc(N1["lo"], 1)
                norm_loop(pool, own_parts)

            @block.vector
            def _(v):
                ch = Chain(v, N1["v"])
                ch.link(v.tensor_scalar(dinv[:], degree[:], 1.0, None, ALU.add))
                v.tensor_scalar(dinv[:], dinv[:], 1.0, None, ALU.max).then_inc(N1["sq"], 1)
                v.wait_ge(N1["sq"], 2)
                ch.link(v.reciprocal(dinv[:], dinv[:]))
                ch.link(v.tensor_scalar(inv_dst[:], degree[:], 1.0, None, ALU.max))
                ch.link(v.reciprocal(inv_dst[:], inv_dst[:]))
                v.tensor_reduce(most[:, 0:1], degree[:], mybir.AxisListType.X, ALU.max).then_inc(N1["mx"], 1)
                v.wait_ge(N1["mt"], 1)
                ch.link(v.tensor_reduce(most[0:1, 1:2], bMost[0:1, 0:P], mybir.AxisListType.X, ALU.max))
                ch.link(v.tensor_scalar(most[0:1, 2:3], most[0:1, 1:2], float(EXACT), None, ALU.is_gt))
                ch.link(v.tensor_copy(many[:], most[0:1, 2:3]))
                v.wait_ge(N1["wt"], 48)
                v.wait_ge(n_t[0], 32)
                first, per = ch.n, 3 * TB + 3

                def means(b):
                    ch.start(first + b * per)
                    inv = inv_src[:, bass.ds(b * TB, TB)]
                    number = tab[:, bass.ds(b * TB, TB), D:D + 1].rearrange("p a o -> p (a o)")
                    ch.link(v.tensor_scalar(inv, number, 1.0, None, ALU.max))
                    stand_alone(v, s_up)
                    ch.link(v.reciprocal(inv, inv))
                    for i in range(TB):
                        n = b * TB + i
                        ch.note(v.scalar_tensor_tensor(tmp[:, i], flat(tab, n)[:, 0:D], inv_src[:, bass.ds(n, 1)],
                                                       flat(own, n), ALU.mult, ALU.add))
                    ch.settle()
                    for i in range(TB):
                        ch.note(v.bn_stats(stats[:, i], tmp[:, i]))
                    ch.settle()
                    stand_alone(v, s_up)
                    for i in range(TB):
                        ch.note(v.bn_aggr(mv[:, i], stats[:, i]))
                    ch.settle()
                    v.tensor_scalar(rstd[:], mv[:, :, 1:2].rearrange("p a o -> p (a o)"), EPS, None, ALU.add
                                    ).then_inc(N1["sq"], 1)

                def own_parts(b):
                    for i in range(TB):
                        m = b * TB + i
                        d = dinv[:, bass.ds(m, 1)]
                        v.wait_ge(N1["rm"], m + 1)
                        v.scalar_tensor_tensor(tmp2[:, i], bU[i][:, D:2 * D], d, bias_l[:, 1],
                                               ALU.mult, ALU.add).then_inc(N1["v2"], 1)
                        v.scalar_tensor_tensor(flat(R, m), bU[i][:, 0:D], d, bias_l[:, 0], ALU.mult, ALU.add
                                               ).then_inc(N1["r"], 1)

                def norms(b):
                    v.wait_ge(N1["sq"], 2 * b + 4)
                    stand_alone(v, s_up)
                    ch.link(v.reciprocal(rstd[:], rstd[:]))
                    for i in range(TB):
                        wait(v, N1["lo"], (b - 1) * TB + i + 1)
                        v.tensor_scalar(hst[:, i], tmp[:, i], mv[:, i, 0:1], rstd[:, i:i + 1],
                                        ALU.subtract, ALU.mult).then_inc(N1["h"], 1)

                means(0)
                norms(0)
                v.wait_ge(n_t[1], 32 * (B - 1))
                with v.Fori(1, B) as b:
                    means(b)
                    own_parts(b - 1)
                    ch.start(first + b * per)
                    ch.n = per - 1
                    norms(b)
                own_parts(B - 1)

        ring = sb("ring", [P, B, TB, NW])
        S = {n: sem("a_" + n) for n in "wt pc g ev lin tr xt rm r h cp sq vc v2 vt".split()}
        s_A = [sem(f"a_A{i}") for i in range(B)]
        wview = lambda W: W.rearrange("(k p) n -> p k n", p=P)

        with ExitStack() as ac:
            aggT = sb("aggT", [P, KD, BW], c=ac)
            tmp = sb("tmp1", [P, D], c=ac)

            PLAN = [[("lin", 0)], [("lin", 1)], [("tr", 0)], [("lin", 2), ("rm", 0)], [("tr", 1)],
                    [("lin", 3), ("rm", 1)], [("tr", 2)], [("lin", 4), ("rm", 2)], [("tr", 3)],
                    [("rm", 3), ("tr", 4)], [("rm", 4)]]

            def aggregate(k, kind, src, dst, w_left, w_right, b_right):
                b_off, t_off = k * B, k * T
                UW = 2 * D if kind == "gcn" else D
                norm = kind != "sage"
                links = {"gcn": 6, "sage": 1, "last": 5}[kind]
                links_off = sum(T * n for n in (6, 1, 1)[:k])
                roots_off = 2 * T * min(k, 1)
                Xh, Xl, Yh, Yl = high[src], low[src], high[dst], low[dst]
                banks, bU, bV = psum[0:4], psum[4:6], psum[6:8]
                with nc.Block() as block:
                    @block.sync
                    def _(sp):
                        def body(hb, k=k):
                            m = HB * k + hb
                            for i in range(B):
                                if i < B - 1:
                                    wait(sp, S["pc"], (m - 1) * (B - 1) + i + 1)
                                else:
                                    wait(sp, S["g"], 2 * m)
                                sp.dma_start(ring[:, i], counts_v[bass.ds(hb, 1), :, TB * i:TB * (i + 1), :]
                                             .rearrange("b p a c -> p (b a) c")).then_inc(s_A[i], 16)
                        if k == 0:
                            body(0)
                        with sp.Fori(1, HB) as hb:
                            body(hb)
                        if k < 3:
                            body(0, k + 1)

                    @block.tensor
                    def _(pe):
                        def tile_steps(b, i, what):
                            n = t_off + (b - 1) * TB + i
                            before = 1 if i == 0 else 2
                            if what == "lin":
                                wait(pe, S["h"], n - before + 1)
                                for h in range(KD):
                                    mm = pe.matmul(bU[i % 2][:, 0:UW], aggT[:, h, i * P:(i + 1) * P],
                                                   w_l[:, h, 0:UW], start=(h == 0), stop=(h == KD - 1))
                                mm.then_inc(S["lin"], 1)
                            elif what == "tr":
                                pe.wait_ge(S["h"], n + 1)
                                wait(pe, S["r"], n - before + 1)
                                for h in range(KD):
                                    mm = pe.transpose(bV[i % 2][:, h * P:(h + 1) * P],
                                                      hst[:, i, h * P:(h + 1) * P], ident[:])
                                mm.then_inc(S["tr"], 1)
                            else:
                                pe.wait_ge(S["xt"], n + 1)
                                for h in range(KD):
                                    mm = pe.matmul(bV[i % 2][:, D:2 * D], hT[:, i % 2, h], w_r[:, h],
                                                   start=(h == 0), stop=(h == KD - 1))
                                mm.then_inc(S["rm"], 1)

                        def sums(b, w, i, dt):
                            pe.wait_ge(s_A[i], 16 * (2 * (b_off + b) + w + 1))
                            for a in range(TB):
                                for h in range(KD):
                                    q = 2 * w + h
                                    first, last = i == 0 and a == 0, i == B - 1 and a == TB - 1
                                    if first:
                                        wait(pe, S["ev"], 4 * (b_off + b - 1) + q + 1)
                                    for part in (Xh, Xl):
                                        mm = pe.matmul(banks[q][:, 0:NW],
                                                       part[:, TB * i + a, h * P:(h + 1) * P].bitcast(dt),
                                                       ring[:, i, a].bitcast(dt),
                                                       start=first and part is Xh, stop=last and part is Xl)
                                    if last:
                                        mm.then_inc(S["g"], 1)
                            if i < B - 1:
                                mm.then_inc(S["pc"], 1)

                        def body(b, front, back, dt):
                            if back:
                                pe.wait_ge(S["wt"], 48 * (k + 1))
                                pe.wait_ge(S["ev"], 4 * (b_off + b))
                            for piece, steps in enumerate(PLAN):
                                if front and piece < HB:
                                    sums(b, piece // B, piece % B, dt)
                                if back:
                                    for what, i in steps:
                                        tile_steps(b, i, what)

                        def blocks(dt):
                            body(0, True, False, dt)
                            body(1, True, True, dt)
                            with pe.Fori(2, B) as b:
                                body(b, True, True, dt)
                            body(B, False, True, dt)

                        exact = pe.value_load(many[0:1, 0:1], min_val=0, max_val=1)
                        with pe.If(exact < 1):
                            blocks(F32R)
                        with pe.Else():
                            blocks(F32)

                    @block.scalar
                    def _(act):
                        act.dma_start(w_l[:, :, 0:UW], w_left).then_inc(S["wt"], 16)
                        act.dma_start(w_r[:], w_right).then_inc(S["wt"], 16)
                        act.dma_start(bias_r[:], b_right.broadcast_to([P, D])).then_inc(S["wt"], 16)

                        def copies(b, quarters):
                            wait(act, S["lin"], t_off + TB * b)
                            for q in quarters:
                                act.wait_ge(S["g"], 4 * (b_off + b) + q + 1)
                                w, h = q // 2, q % 2
                                act.copy(aggT[:, h, w * NW:(w + 1) * NW], banks[q][:, 0:NW]).then_inc(S["ev"], 1)

                        def body(b, front, back):
                            if back:
                                for i in range(B + 1):
                                    if i == B and front:
                                        copies(b, (0, 1))
                                    n = t_off + (b - 1) * TB + i
                                    t = (b - 1) * TB + i
                                    if i < B:
                                        if norm:
                                            act.wait_ge(S["sq"], roots_off + 2 * t + 1)
                                            act.activation(rstd[:, i:i + 1], rstd[:, i:i + 1], ACT.Sqrt
                                                           ).then_inc(S["sq"], 1)
                                        act.wait_ge(S["h"], n + 1)
                                        if kind == "gcn":
                                            act.copy(flat(own, t), hst[:, i])
                                        if kind == "last":
                                            act.copy(flat(own, t), hst[:, i]).then_inc(S["cp"], 1)
                                        else:
                                            act.copy(flat(Yh, t).bitcast(F32R), hst[:, i]).then_inc(S["cp"], 1)
                                    if i >= 1:
                                        act.wait_ge(S["tr"], n)
                                        wait(act, S["rm"], n - 1 if i == 1 else n - 2)
                                        act.copy(hT[:, (i - 1) % 2],
                                                 bV[(i - 1) % 2][:, 0:D].rearrange("p (k n) -> p k n", k=KD)
                                                 ).then_inc(S["xt"], 1)
                            if front:
                                if not back:
                                    copies(b, (0, 1))
                                copies(b, (2, 3))
                        body(0, True, False)
                        body(1, True, True)
                        with act.Fori(2, B) as b:
                            body(b, True, True)
                        body(B, False, True)

                    @block.vector
                    def _(v):
                        ch, rch = Chain(v, S["vc"]), Chain(v, S["v2"])
                        v.wait_ge(S["wt"], 48 * (k + 1))

                        def body(b):
                            for i in range(B + 2):
                                n = t_off + (b - 1) * TB + i
                                t = (b - 1) * TB + i
                                if i < B:
                                    U, out_t = bU[i % 2], hst[:, i]
                                    ch.start(links_off + t * links)
                                    v.wait_ge(S["lin"], n + 1)
                                    wait(v, S["tr"], n - TB + 1)
                                    wait(v, S["cp"], n - TB + 1)
                                    wait(v, S["vt"], n - TB + 1)
                                    wait(v, S["h"], n)
                                    if kind == "gcn":
                                        d = dinv[:, bass.ds(t, 1)]
                                        ch.link(v.scalar_tensor_tensor(tmp[:], U[:, 0:D], d, flat(R, t),
                                                                       ALU.mult, ALU.add))
                                        ch.link(v.scalar_tensor_tensor(out_t, U[:, D:2 * D], d, flat(own, t),
                                                                       ALU.mult, ALU.add))
                                        ch.link(v.scalar_tensor_tensor(tmp[:], tmp[:], 0.0, out_t, ALU.max, ALU.add))
                                    else:
                                        ch.link(v.scalar_tensor_tensor(tmp[:], U[:, 0:D], inv_dst[:, bass.ds(t, 1)],
                                                                       flat(R, t), ALU.mult, ALU.add))
                                        if kind == "last":
                                            ch.link(v.tensor_tensor(tmp[:], tmp[:], flat(own, t), ALU.add))
                                    if norm:
                                        ch.link(v.bn_stats(stats[:, i], tmp[:]))
                                        stand_alone(v, s_up)
                                        ch.link(v.bn_aggr(mv[:, i], stats[:, i]))
                                        v.tensor_scalar(rstd[:, i:i + 1], mv[:, i, 1:2], EPS, None, ALU.add
                                                        ).then_inc(S["sq"], 1)
                                        v.wait_ge(S["sq"], roots_off + 2 * t + 2)
                                        stand_alone(v, s_up)
                                        ch.link(v.reciprocal(rstd[:, i:i + 1], rstd[:, i:i + 1]))
                                        v.tensor_scalar(out_t, tmp[:], mv[:, i, 0:1], rstd[:, i:i + 1],
                                                        ALU.subtract, ALU.mult).then_inc(S["h"], 1)
                                    else:
                                        v.tensor_scalar(out_t, tmp[:], 0.0, None, ALU.max).then_inc(S["h"], 1)
                                    assert ch.n == links
                                if i >= 2:
                                    t, j = t - 2, i - 2
                                    V = bV[j % 2][:, D:2 * D]
                                    v.wait_ge(S["cp"], n - 1)
                                    v.wait_ge(S["rm"], n - 1)
                                    if kind == "last":
                                        rch.start(2 * t)
                                        v.tensor_tensor(flat(Yh, t).bitcast(F32R), V, bias_r[:], ALU.add
                                                        ).then_inc(S["v2"], 1)
                                        wait(v, S["tr"], n - 1)
                                        v.tensor_tensor(hst[:, j], V, bias_r[:], ALU.add).then_inc(S["v2"], 1)
                                        v.wait_ge(S["v2"], 2 * t + 2)
                                        v.tensor_tensor(flat(Yl, t).bitcast(F32R), hst[:, j], flat(Yh, t),
                                                        ALU.subtract).then_inc(S["vt"], 1)
                                        v.wait_ge(S["vt"], n - 1)
                                        v.sem_inc(S["r"])
                                    else:
                                        v.tensor_tensor(flat(Yl, t).bitcast(F32R), hst[:, j], flat(Yh, t),
                                                        ALU.subtract).then_inc(S["vt"], 1)
                                        v.tensor_tensor(flat(R, t), V, bias_r[:], ALU.add).then_inc(S["r"], 1)
                        body(1)
                        with v.Fori(2, B) as b:
                            body(b)
                        body(B)

            aggregate(0, "gcn", 0, 1, wview(gW), wview(Wr[0]), bl[0])
            aggregate(1, "sage", 1, 0, wview(Wl[0]), wview(Wr[1]), bl[1])
            aggregate(2, "sage", 0, 1, wview(Wl[1]), wview(Wr[2]), bl[2])
            aggregate(3, "last", 1, 0, wview(Wl[2]), wview(W3), b3)

        with ExitStack() as fc:
            tmp = sb("tmp2", [P, 2, D], c=fc)
            f = {n: sem("f_" + n, fc) for n in "tr ev mm vc sq h rd".split()}
            f_A = [sem(f"f_A{i}", fc) for i in range(2)]
            f_o = [sem(f"f_o{i}", fc) for i in range(2)]
            rows = ring[:].rearrange("p s a c -> p (s a c)")[:, 0:2 * NP].rearrange("p (s c) -> p s c", s=2)
            half = lambda X: X[:].rearrange("p a c -> p (a c)")[:, 0:T * P].rearrange("p (s n) -> p s n", s=T)
            AT_exact = [half(high[1]), half(low[1])]
            R_all = R[:].rearrange("p a c -> p (a c)").rearrange("p (z s n) -> p z s n", z=2, s=T)
            AT_full = [R_all[:, 0], R_all[:, 1]]
            QN = (T + 3) // 4
            rows_v = counts_v.rearrange("b p a c -> p a b c")
            bU = psum[4:6]
            block = fc.enter_context(nc.Block())

            def pairs(eng, body):
                body(0, 0)
                body(1, 1)
                with eng.Fori(1, T // 2) as h:
                    body(2 * h, 0)
                    body(2 * h + 1, 1)
                body(T - 1, 0)

            @block.sync
            def _(sp):
                def load(n, z):
                    wait(sp, f["tr"], QN * (n - 1))
                    sp.dma_start(rows[:, z].rearrange("p (b c) -> p b c", b=HB),
                                 rows_v[:, bass.ds(n, 1), :, :].rearrange("p a b c -> p (a b) c")
                                 ).then_inc(f_A[z], 16)

                pairs(sp, load)

            @block.gpsimd
            def _(pool):
                def store(n, z):
                    pool.wait_ge(f["h"], n + 1)
                    pool.dma_start(out_v[:, bass.ds(n, 1), :].rearrange("p a c -> p (a c)"),
                                   hst[0:NODES // T, z]).then_inc(f_o[z], 16)
                pairs(pool, store)
                pool.wait_ge(f_o[0], 16 * (T // 2 + 1))
                pool.wait_ge(f_o[1], 16 * (T // 2))

            @block.tensor
            def _(pe):
                def products(n, z, q, AT, dt):
                    if q == 0:
                        pe.wait_ge(f["ev"], QN * (n + 1))
                        wait(pe, f["rd"], n - 1)
                    for s in range(4 * q, min(4 * q + 4, T)):
                        for part in (high[0], low[0]):
                            mm = pe.matmul(bU[z][:, 0:D], AT[z][:, s].bitcast(dt), part[:, s].bitcast(dt),
                                           start=(s == 0 and part is high[0]), stop=(s == T - 1 and part is low[0]))
                    if q == QN - 1:
                        mm.then_inc(f["mm"], 1)

                def turn(n, z, q):
                    if q == 0:
                        if isinstance(n, int):
                            pe.wait_ge(f_A[z], 16 * (n // 2 + 1))
                    wait(pe, f["ev"], QN * n + (q - 2 if q < 3 else q - 3))
                    for s in range(4 * q, min(4 * q + 4, T)):
                        mm = pe.transpose(psum[q % 4][:, (s - 4 * q) * P:(s - 4 * q + 1) * P],
                                          rows[:, z, s * P:(s + 1) * P], ident[:])
                    mm.then_inc(f["tr"], 1)

                def tiles(AT, dt):
                    def body(n, z, before=True):
                        for q in range(QN):
                            turn(n, z, q)
                            if before:
                                products(n - 1, 1 - z, q, AT, dt)
                    body(0, 0, False)
                    body(1, 1)
                    with pe.Fori(1, T // 2) as h:
                        pe.wait_ge(f_A[0], 16 * (h + 1))
                        body(2 * h, 0)
                        pe.wait_ge(f_A[1], 16 * (h + 1))
                        body(2 * h + 1, 1)
                    body(T - 1, 0)
                    for q in range(QN):
                        products(T - 1, 0, q, AT, dt)

                exact = pe.value_load(many[0:1, 0:1], min_val=0, max_val=1)
                with pe.If(exact < 1):
                    tiles(AT_exact, F32R)
                with pe.Else():
                    tiles(AT_full, F32)

            @block.scalar
            def _(act):
                def tiles(AT, dt):
                    def root(n, z):
                        act.wait_ge(f["sq"], 2 * n + 1)
                        act.activation(rstd[:, z:z + 1], rstd[:, z:z + 1], ACT.Sqrt).then_inc(f["sq"], 1)

                    def body(n, z):
                        for q in range(QN):
                            w = min(4, T - 4 * q)
                            act.wait_ge(f["tr"], QN * n + q + 1)
                            if q == 0:
                                wait(act, f["mm"], n - 1)
                            act.copy(AT[z][:, 4 * q:4 * q + w].bitcast(dt),
                                     psum[q % 4][:, 0:w * P].rearrange("p (s n) -> p s n", s=w)).then_inc(f["ev"], 1)
                        if not isinstance(n, int) or n >= 2:
                            root(n - 2, z)
                    pairs(act, body)
                    root(T - 2, 1)
                    root(T - 1, 0)

                exact = act.value_load(many[0:1, 0:1], min_val=0, max_val=1)
                with act.If(exact < 1):
                    tiles(AT_exact, F32R)
                with act.Else():
                    tiles(AT_full, F32)

            @block.vector
            def _(v):
                ch = Chain(v, f["vc"])

                def body(n, z):
                    ch.start(n * 3)
                    v.wait_ge(f["mm"], n + 1)
                    wait(v, f["h"], n - 1)
                    v.scalar_tensor_tensor(tmp[:, z], bU[z][:, 0:D], inv_src[:, bass.ds(n, 1)], flat(own, n),
                                           ALU.mult, ALU.add).then_inc(f["rd"], 1)
                    v.wait_ge(f["rd"], n + 1)
                    ch.link(v.bn_stats(stats[:, z], tmp[:, z]))
                    stand_alone(v, s_up)
                    ch.link(v.bn_aggr(mv[:, z], stats[:, z]))
                    v.tensor_scalar(rstd[:, z:z + 1], mv[:, z, 1:2], EPS, None, ALU.add).then_inc(f["sq"], 1)
                    v.wait_ge(f["sq"], 2 * n + 2)
                    stand_alone(v, s_up)
                    ch.link(v.reciprocal(rstd[:, z:z + 1], rstd[:, z:z + 1]))
                    if not isinstance(n, int) or n >= 2:
                        v.wait_ge(f_o[z], 16 * (n // 2) if isinstance(n, int) else 16 * steps[0])
                    v.tensor_scalar(hst[:, z], tmp[:, z], mv[:, z, 0:1], rstd[:, z:z + 1],
                                    ALU.subtract, ALU.mult).then_inc(f["h"], 1)
                steps = [None]
                body(0, 0)
                body(1, 1)
                with v.Fori(1, T // 2) as h:
                    steps[0] = h
                    body(2 * h, 0)
                    body(2 * h + 1, 1)
                body(T - 1, 0)


def kernel(x, src, dst, edge_attr_128, **w):
    import numpy as np
    import concourse.bacc as bacc
    from concourse.bass_utils import run_bass_kernel_spmd

    def padded(a, shape):
        o = np.zeros(shape, a.dtype)
        o[tuple(slice(0, s) for s in a.shape)] = a
        return o

    def edges(a):
        o = np.full(EP, NP - 1, np.int32)
        o[:a.shape[0]] = np.asarray(a)
        return np.ascontiguousarray(o.reshape(G * GC, C).T)

    w = {k: np.asarray(v) for k, v in w.items()}
    xp = padded(np.asarray(x), (NP, D))
    W0 = padded(w["L0_gnn_W0"], (2 * D, H1))
    W1 = padded(w["L0_gnn_W1"], (H1, H2))
    W2b = np.concatenate([w["L0_gnn_W2"], w["L0_gnn_b2"][None]])
    arrays = {
        "xT": np.ascontiguousarray(xp.T),
        "x": xp,
        "src_col": edges(src),
        "dst_col": edges(dst),
        "edge_T": padded(np.asarray(edge_attr_128).T, (P, EP)),
        "W0": W0, "b0": padded(w["L0_gnn_b0"][None], (1, H1)),
        "W1": W1, "b1": np.ascontiguousarray(padded(w["L0_gnn_b1"], (H2,)).reshape(H2T, H2P).T),
        "W2b": W2b, "Wg": w["L0_gnn_Wg"],
        "gW": np.concatenate([w["L1_gnn_W1"], w["L1_gnn_W2"]], axis=1),
        "gb1": w["L1_gnn_b1"][None], "gb2": w["L1_gnn_b2"][None],
    }
    for i in (1, 2, 3):
        arrays[f"Wl{i}"] = np.ascontiguousarray(w[f"L2_gnn_W{i}l"].T)
        arrays[f"Wr{i}"] = np.ascontiguousarray(w[f"L2_gnn_W{i}r"].T)
        arrays[f"bl{i}"] = w[f"L2_gnn_b{i}l"][None]
    arrays["W3"], arrays["b3"] = w["L3_gnn_W"], w["L3_gnn_b"][None]
    nc = bacc.Bacc("TRN2", target_bir_lowering=False, num_devices=1)
    a = {n: nc.dram_tensor("in_" + n, v.shape, mybir.dt.from_np(v.dtype), kind="ExternalInput").ap()
         for n, v in arrays.items()}
    out = nc.dram_tensor("out", (NODES, D), F32, kind="ExternalOutput").ap()
    build(nc, a["xT"], a["x"], a["src_col"], a["dst_col"], a["edge_T"], a["W0"], a["b0"], a["W1"], a["b1"],
          a["W2b"], a["Wg"], a["gW"], a["gb1"], a["gb2"], [a["Wl1"], a["Wl2"], a["Wl3"]],
          [a["bl1"], a["bl2"], a["bl3"]], [a["Wr1"], a["Wr2"], a["Wr3"]], a["W3"], a["b3"], out)
    r = run_bass_kernel_spmd(nc, [{"in_" + n: v for n, v in arrays.items()}], core_ids=[0])
    return r.results[0]["out"]
```
